# Optimizing a Trainium2 kernel written in Bass

```python
import numpy as np
import jax
import jax.numpy as jnp

def _softmax(x, axis=-1):
    return jax.nn.softmax(x, axis=axis)

def _gelu(x):
    return jax.nn.gelu(x, approximate=True)

def _silu(x):
    return jax.nn.silu(x)

def _sigmoid(x):
    return jax.nn.sigmoid(x)

def _layernorm(x, axis=-1, eps=1e-05):
    m = jnp.mean(x, axis=axis, keepdims=True)
    v = jnp.var(x, axis=axis, keepdims=True)
    return (x - m) / jnp.sqrt(v + eps)

def _scatter_add(tgt, idx, src, axis=0):
    return tgt.at[idx].add(src)

def _segment_sum(src, seg, n):
    return jax.ops.segment_sum(src, seg, n)
kernel_name = 'mk_gnn_resnorm_d1_gnn_r32_c0aa4b'

def setup_inputs(seed: int=0):
    np.random.seed(seed)
    _w = jnp.asarray

    def _rec_inputs():
        import jax
        import jax.numpy as jnp
        _gk = jax.random.key(seed)
        x = -0.0003713 + 1 * jax.random.normal(jax.random.fold_in(_gk, 1), (3125, 128), jnp.float32)
        _s = jax.random.randint(jax.random.fold_in(_gk, 2), (50000,), 0, 3125, jnp.int32)
        _d = jax.random.randint(jax.random.fold_in(_gk, 3), (50000,), 0, 3125, jnp.int32)
        _loop = jnp.arange(3125, dtype=jnp.int32)
        src = jnp.concatenate([_s, _d, _loop])
        dst = jnp.concatenate([_d, _s, _loop])
        _o = jnp.argsort(dst, stable=True)
        src = src[_o]
        dst = dst[_o]
        edge_attr_64 = 0.000102155 + 1.00015 * jax.random.normal(jax.random.fold_in(_gk, 11), (103125, 64), jnp.float32)
        edge_weight = jax.random.uniform(jax.random.fold_in(_gk, 13), (103125,), jnp.float32, 0.0, 0.999999)
        return (x, src, dst, edge_attr_64, edge_weight)
    x, src, dst, edge_attr_64, edge_weight = _rec_inputs()

    def _L0_gnn_setup():
        import jax, jax.numpy as jnp
        import numpy as np
        N_NODES = 3125
        N_EDGES = 15625
        IN_CH = 128
        EDGE_CH = 64

        def _glorot(key, shape):
            fan_in, fan_out = (shape[0], shape[1])
            lim = (6.0 / (fan_in + fan_out)) ** 0.5
            return jax.random.uniform(key, shape, jnp.float32, -lim, lim)
        key = jax.random.key(seed)
        ks = jax.random.split(key, 14)
        x = jax.random.normal(ks[0], (N_NODES, IN_CH), jnp.float32)
        edge_index = jax.random.randint(ks[1], (2, N_EDGES), 0, N_NODES, jnp.int64)
        edge_attr = jax.random.normal(ks[2], (N_EDGES, EDGE_CH), jnp.float32)
        timestamps = jax.random.uniform(ks[3], (N_EDGES,), jnp.float32)
        We1 = _glorot(ks[4], (EDGE_CH, 2 * EDGE_CH))
        be1 = jnp.zeros((2 * EDGE_CH,), jnp.float32)
        We2 = _glorot(ks[5], (2 * EDGE_CH, IN_CH))
        be2 = jnp.zeros((IN_CH,), jnp.float32)
        Wt = _glorot(ks[6], (1, IN_CH))
        bt = jnp.zeros((IN_CH,), jnp.float32)
        Wn1 = _glorot(ks[7], (2 * IN_CH, IN_CH))
        bn1 = jnp.zeros((IN_CH,), jnp.float32)
        Wn2 = _glorot(ks[8], (IN_CH, IN_CH))
        bn2 = jnp.zeros((IN_CH,), jnp.float32)
        return {'x': x, 'edge_index': edge_index, 'edge_attr': edge_attr, 'timestamps': timestamps, 'We1': We1, 'be1': be1, 'We2': We2, 'be2': be2, 'Wt': Wt, 'bt': bt, 'Wn1': Wn1, 'bn1': bn1, 'Wn2': Wn2, 'bn2': bn2}
    _L0_gnn_all = _L0_gnn_setup()
    _L0_gnn_in = {k: v for k, v in _L0_gnn_all.items() if k in ('We1', 'be1', 'We2', 'be2', 'Wt', 'bt', 'Wn1', 'bn1', 'Wn2', 'bn2')}
    del _L0_gnn_all
    return {'x': x, 'src': src, 'dst': dst, 'edge_attr_64': edge_attr_64, 'edge_weight': edge_weight, 'L0_gnn_We1': _L0_gnn_in['We1'], 'L0_gnn_be1': _L0_gnn_in['be1'], 'L0_gnn_We2': _L0_gnn_in['We2'], 'L0_gnn_be2': _L0_gnn_in['be2'], 'L0_gnn_Wt': _L0_gnn_in['Wt'], 'L0_gnn_bt': _L0_gnn_in['bt'], 'L0_gnn_Wn1': _L0_gnn_in['Wn1'], 'L0_gnn_bn1': _L0_gnn_in['bn1'], 'L0_gnn_Wn2': _L0_gnn_in['Wn2'], 'L0_gnn_bn2': _L0_gnn_in['bn2']}

def reference(x, src, dst, edge_attr_64, edge_weight, L0_gnn_We1, L0_gnn_be1, L0_gnn_We2, L0_gnn_be2, L0_gnn_Wt, L0_gnn_bt, L0_gnn_Wn1, L0_gnn_bn1, L0_gnn_Wn2, L0_gnn_bn2):
    import jax
    import jax.numpy as jnp

    def _L0_gnn_ref(x, edge_index, edge_attr, timestamps, We1, be1, We2, be2, Wt, bt, Wn1, bn1, Wn2, bn2):
        import jax, jax.numpy as jnp
        import numpy as np
        N_NODES = 3125
        N_EDGES = 15625
        IN_CH = 128
        EDGE_CH = 64

        def _glorot(key, shape):
            fan_in, fan_out = (shape[0], shape[1])
            lim = (6.0 / (fan_in + fan_out)) ** 0.5
            return jax.random.uniform(key, shape, jnp.float32, -lim, lim)
        ts = timestamps[:, None]
        ef = jax.nn.relu(edge_attr @ We1 + be1) @ We2 + be2
        tw = jax.nn.sigmoid(ts @ Wt + bt)
        ef = ef * tw
        row, col = (edge_index[0], edge_index[1])
        combined = jnp.concatenate([x[row], ef], axis=1)
        msg = jax.nn.relu(combined @ Wn1 + bn1) @ Wn2 + bn2
        out = jax.ops.segment_sum(msg, col, num_segments=x.shape[0])
        return out + x
    edge_index = jnp.stack([src, dst])
    x = _layernorm(x + _L0_gnn_ref(x, edge_index, edge_attr_64, edge_weight, L0_gnn_We1, L0_gnn_be1, L0_gnn_We2, L0_gnn_be2, L0_gnn_Wt, L0_gnn_bt, L0_gnn_Wn1, L0_gnn_bn1, L0_gnn_Wn2, L0_gnn_bn2), axis=-1)
    return x

_drawn_inputs = setup_inputs


def setup_inputs(seed=0):
    import zlib

    import numpy as np

    out = dict(_drawn_inputs(seed))
    spreads = {'L0_gnn_be1': (0.0, 0.1),
     'L0_gnn_be2': (0.0, 0.1),
     'L0_gnn_bt': (0.0, 0.671),
     'L0_gnn_bn1': (0.0, 0.1),
     'L0_gnn_bn2': (0.0, 0.1)}
    factors = {'edge_weight': 8.0, 'L0_gnn_Wt': 7.968}
    for name, (base, spread) in spreads.items():
        noise = np.random.default_rng([zlib.crc32(name.encode()), seed]).standard_normal(out[name].shape)
        drawn = base * np.exp(spread * noise) if base else spread * noise
        out[name] = jnp.asarray(drawn.astype(out[name].dtype))
    for name, factor in factors.items():
        out[name] = (out[name] * factor).astype(out[name].dtype)
    return out
```

```python
import numpy as np

import concourse.bass as bass
from concourse import mybir
from contextlib import ExitStack

F32 = mybir.dt.float32
BF16 = mybir.dt.bfloat16
I32 = mybir.dt.int32
ALU = mybir.AluOpType
ACT = mybir.ActivationFunctionType
AXX = mybir.AxisListType.X

P = 128
N_NODES = 3125
N_EDGES = 103125
F = 128
EF = 64
NT = 25
NPAD = P * NT
TPC = 4
C = TPC * P
NCH = -(-N_EDGES // (2 * C)) * 2
NTILES = -(-N_EDGES // P)
EPAD = NCH * C
U = 4
W = 32
WW = 448
NW = -(-(N_NODES + 1) // WW)
EPS = 1e-5
LEAD = 3
TURNS = (NCH - LEAD) // U


def tiles_of(c):
    return min(TPC, NTILES - c * TPC) if isinstance(c, int) else TPC


def wait_count(eng, sem, value):
    if not isinstance(value, int) or value > 0:
        eng.wait_ge(sem, value)


def main_steps(eng, step):
    for k in range(-LEAD, U):
        step(k // U, k % U)
    with eng.Fori(1, TURNS) as turn:
        for u in range(U):
            step(turn, u)
    for k in range(TURNS * U, NCH):
        step(k // U, k % U)


def gnn_kernel(nc, x, xT, src, dst, dst_rows, edge_attr, edge_weight, We1, be1, We2, be2, Wt, bt,
               Wn1, bn1, Wn2, bn2, out):
    table = nc.dram_tensor("table", [NPAD, F], F32, kind="Internal").ap()
    span_dram = nc.dram_tensor("span_dram", [2, NCH], F32, kind="Internal").ap()

    with ExitStack() as ctx:
        def sb(name, shape, dt=F32):
            return ctx.enter_context(nc.sbuf_tensor(name, shape, dt))

        def sem(name):
            return ctx.enter_context(nc.semaphore(name))

        we1 = sb("we1", [P, F])
        we2 = sb("we2", [P, F])
        wn1x = sb("wn1x", [P, F])
        wn1e = sb("wn1e", [P, F])
        wn2 = sb("wn2", [P, F])
        be1c = sb("be1c", [P, 1])
        be2c = sb("be2c", [P, 1])
        wtc = sb("wtc", [P, 1])
        btc = sb("btc", [P, 1])
        bn1r = sb("bn1r", [1, F])
        bn2r = sb("bn2r", [1, F])
        ones_row = sb("ones_row", [1, P])
        ones_bf = sb("ones_bf", [P, P], BF16)
        xT_sb = sb("xT_sb", [P, NPAD])
        x_sb = sb("x_sb", [P, NT * F])
        xw = sb("xw", [P, NT * F])
        y = sb("y", [P, NT * F])
        dst_i = sb("dst_i", [P, NCH * TPC], I32)
        dst_f = sb("dst_f", [P, NCH * TPC])
        dst_rel = sb("dst_rel", [P, NCH * TPC])
        dst_ci = sb("dst_ci", [NCH // 2, 2, C], I32)
        lo_c = sb("lo_c", [NCH // 2, 2])
        hi_c = sb("hi_c", [NCH // 2, 2])
        lo_b = sb("lo_b", [P, NCH])
        hi_b = sb("hi_b", [P, NCH])
        span = sb("span", [P, NCH])
        base_i = sb("base_i", [P, NCH], I32)
        widest = sb("widest", [P, 1])
        narrow_i = sb("narrow_i", [P, 1], I32)
        iota_i = sb("iota_i", [P, NW * WW], I32)
        iota_f = sb("iota_f", [P, NW * WW])
        idx = sb("idx", [P, 2, 2 * TPC], I32)
        ea = sb("ea", [P, 2, C])
        ew = sb("ew", [P, U, C])
        gath = sb("gath", [P, U, C])
        h1 = sb("h1", [P, 2, C])
        tw = sb("tw", [P, 2, C])
        ef = sb("ef", [P, 2, C])
        pre = sb("pre", [P, 2, C])
        r = sb("r", [P, 2, C])
        hot = sb("hot", [P, 2, TPC, W])
        hot_wide = sb("hot_wide", [P, 2, WW])
        acc = sb("acc", [P, 2, NPAD])
        stats = sb("stats", [P, NT, nc.vector.BN_STATS_DIM])
        mv = sb("mv", [P, NT, 2])
        std = sb("std", [P, NT])
        rstd = sb("rstd", [P, NT])
        eps = sb("eps", [P, 1])

        ps = ctx.enter_context(nc.psum_tensor("ps", [P, 8, 512], F32))
        ps_a, ps_b, ps_c, ps_d = (ps[:, 2 * n:2 * n + 2, :] for n in range(4))

        w_in = sem("w_in")
        x_in = sem("x_in")
        dst_in = sem("dst_in")
        consts = sem("consts")
        iota_done = sem("iota_done")
        acc_zero = sem("acc_zero")
        xw_ready = sem("xw_ready")
        xw_copied = sem("xw_copied")
        table_out = sem("table_out")
        span_ready = sem("span_ready")
        span_out = sem("span_out")
        span_in = sem("span_in")
        dve_prep = sem("dve_prep")
        flag_ready = sem("flag_ready")
        idx_in = [sem(f"idx_in{n}") for n in range(2)]
        ea_in = [sem(f"ea_in{n}") for n in range(2)]
        ew_in = [sem(f"ew_in{n}") for n in range(U)]
        gath_in = [sem(f"gath_in{n}") for n in range(U)]
        slots_granted = sem("slots_granted")
        a_ready = sem("a_ready")
        h1_ready = sem("h1_ready")
        b_ready = sem("b_ready")
        tw_ready = sem("tw_ready")
        ef_ready = sem("ef_ready")
        c_ready = sem("c_ready")
        pre_ready = sem("pre_ready")
        r_ready = sem("r_ready")
        hot_ready = sem("hot_ready")
        d_ready = sem("d_ready")
        acc_done = sem("acc_done")
        wide_ready = sem("wide_ready")
        wide_used = sem("wide_used")
        wide_sum = sem("wide_sum")
        wide_added = sem("wide_added")
        msg_ready = sem("msg_ready")
        y_ready = sem("y_ready")
        mv_ready = sem("mv_ready")
        std_ready = sem("std_ready")
        norm_ready = sem("norm_ready")
        out_done = sem("out_done")

        block = ctx.enter_context(nc.Block())

        src_v = src.rearrange("p (n t) -> p n t", t=2 * TPC)
        ea_v = edge_attr.rearrange("p (n c) -> p n c", c=C)
        x_rows = x.rearrange("(p j) f -> p (j f)", j=NT)
        out_rows = out.rearrange("(p j) f -> p (j f)", j=NT)
        table_rows = table.rearrange("(p j) f -> p (j f)", j=NT)
        groups = [(g, range(g * 4, min(g * 4 + 4, NT))) for g in range(-(-NT // 4))]

        def group_cols(js):
            return slice(js[0] * F, (js[-1] + 1) * F)

        @block.sync
        def _(sp):
            sp.dma_start(xT_sb[:, :], xT).then_inc(x_in, 16)
            sp.dma_start(wn1x[:, :], Wn1[0:F, :]).then_inc(x_in, 16)
            sp.dma_start(bn1r[:, :], bn1.rearrange("(a n) -> a n", a=1)).then_inc(x_in, 16)
            sp.dma_start(dst_ci[:, :, :], dst_rows).then_inc(dst_in, 16)
            sp.dma_start(dst_i[:, :], dst).then_inc(dst_in, 16)

            def load_pair(turn, half, stage_waits):
                pair = turn * (U // 2) + half
                if stage_waits:
                    for slot in (2 * half, 2 * half + 1):
                        sp.wait_ge(gath_in[slot], turn * (16 * TPC))
                sp.dma_start(idx[:, half, :], src_v[:, bass.ds(pair, 1), :]).then_inc(idx_in[half], 16)
                if stage_waits:
                    sp.wait_ge(a_ready, pair * 2 - 2)
                sp.dma_start(ea[:, half, :], ea_v[:, bass.ds(pair, 1), :]).then_inc(ea_in[half], 16)
                for n in range(2):
                    slot, c = 2 * half + n, pair * 2 + n
                    if stage_waits:
                        sp.wait_ge(tw_ready, c - U + 1)
                    sp.dma_start(ew[:, slot, :], edge_weight[:, bass.ds(c * C, C)].partition_broadcast(P)
                                 ).then_inc(ew_in[slot], 16)

            for half in range(U // 2):
                load_pair(0, half, False)
            sp.dma_start(x_sb[:, :], x_rows).then_inc(w_in, 16)
            sp.wait_ge(span_ready, 2)
            for n, part in enumerate((lo_c, hi_c)):
                sp.dma_start(span_dram[n, :].rearrange("(p a) -> p a", a=2), part[:, :]).then_inc(span_out, 16)
            sp.wait_ge(span_out, 32)
            for n, part in enumerate((lo_b, hi_b)):
                sp.dma_start(part[:, :], span_dram[n:n + 1, :].partition_broadcast(P)).then_inc(span_in, 16)
            for g, js in groups:
                sp.wait_ge(xw_copied, g + 1)
                sp.dma_start(table_rows[:, group_cols(js)], xw[:, group_cols(js)]).then_inc(table_out, 16)
            with sp.Fori(1, NCH // U) as turn:
                for half in range(U // 2):
                    load_pair(turn, half, True)
            for pair in range(NCH // U * (U // 2), NCH // 2):
                load_pair(pair // (U // 2), pair % (U // 2), True)
            for g, js in groups:
                sp.wait_ge(norm_ready, js[-1] + 1)
                sp.dma_start(out_rows[:, group_cols(js)], y[:, group_cols(js)]).then_inc(out_done, 16)
            sp.wait_ge(out_done, 16 * len(groups))

        @block.gpsimd
        def _(pool):
            nc.gpsimd.iota(iota_i[:, :], pattern=[[1, NW * WW]], base=0, channel_multiplier=0).then_inc(iota_done, 1)
            nc.gpsimd.memset(acc[:, :, :], 0.0).then_inc(acc_zero, 1)
            pool.wait_ge(table_out, 16 * len(groups))

            def gather(turn, u):
                c = turn * U + u
                half, pair_turn = u // 2, turn
                if u % 2 == 0:
                    pool.wait_ge(idx_in[half], (pair_turn + 1) * 16)
                wait_count(pool, pre_ready, c - U + 1)
                pool.sem_inc(slots_granted, 1)
                tiles = tiles_of(c)
                for t in range(tiles):
                    at = TPC * (u % 2) + t
                    pool.indirect_dma_start(
                        gath[:, u, t * F:(t + 1) * F], None, table,
                        bass.IndirectOffsetOnAxis(idx[:, half, at:at + 1], 0)).then_inc(gath_in[u], 16)

            for u in range(U):
                gather(0, u)
            with pool.Fori(1, NCH // U) as turn:
                for u in range(U):
                    gather(turn, u)
            for c in range(NCH // U * U, NCH):
                gather(c // U, c % U)

        @block.scalar
        def _(act):
            for half in range(2):
                act.dma_start(we1[half * EF:(half + 1) * EF, :], We1).then_inc(w_in, 16)
            act.dma_start(be1c[:, :], be1.rearrange("(p a) -> p a", a=1)).then_inc(w_in, 16)
            act.dma_start(wtc[:, :], Wt.rearrange("a p -> p a")).then_inc(w_in, 16)
            act.dma_start(btc[:, :], bt.rearrange("(p a) -> p a", a=1)).then_inc(w_in, 16)
            act.dma_start(we2[:, :], We2).then_inc(w_in, 16)
            act.dma_start(be2c[:, :], be2.rearrange("(p a) -> p a", a=1)).then_inc(w_in, 16)
            act.dma_start(wn1e[:, :], Wn1[F:2 * F, :]).then_inc(w_in, 16)
            act.dma_start(wn2[:, :], Wn2).then_inc(w_in, 16)
            act.dma_start(bn2r[:, :], bn2.rearrange("(a n) -> a n", a=1)).then_inc(w_in, 16)
            for g, js in groups:
                act.wait_ge(xw_ready, g + 1)
                nc.scalar.activation(xw[:, group_cols(js)], ps[:, g, 0:len(js) * F], ACT.Copy
                                     ).then_inc(xw_copied, 1)
            act.wait_ge(w_in, 11 * 16)

            def step(turn, u):
                k = turn * U + u
                if not isinstance(k, int) or k >= 0:
                    act.wait_ge(pre_ready, k + 1)
                    wait_count(act, d_ready, k - 1)
                    n = tiles_of(k) * F
                    nc.scalar.activation(r[:, u % 2, 0:n], pre[:, u % 2, 0:n], ACT.Relu).then_inc(r_ready, 1)
                c = k + LEAD
                if not isinstance(c, int) or c < NCH:
                    s, t = (u + LEAD) % U, turn + (u + LEAD) // U
                    act.wait_ge(ew_in[s], (t + 1) * 16)
                    wait_count(act, ef_ready, c - 1)
                    nc.scalar.activation(tw[:, s % 2, :], ew[:, s, :], ACT.Sigmoid, bias=btc[:, 0:1],
                                         scale=wtc[:, 0:1]).then_inc(tw_ready, 1)
                    act.wait_ge(a_ready, c + 1)
                    wait_count(act, b_ready, c - 1)
                    nc.scalar.activation(h1[:, s % 2, :], ps_a[:, s % 2, :], ACT.Relu, bias=be1c[:, 0:1]
                                         ).then_inc(h1_ready, 1)

            main_steps(act, step)
            for g, js in groups:
                act.wait_ge(mv_ready, js[-1] + 1)
                nc.scalar.activation(std[:, js[0]:js[-1] + 1], mv[:, js[0]:js[-1] + 1, 1], ACT.Sqrt,
                                     bias=eps[:, 0:1]).then_inc(std_ready, 1)

        @block.tensor
        def _(pe):
            pe.wait_ge(x_in, 48)
            pe.wait_ge(consts, 2)
            xT_v = xT_sb[:, :].rearrange("f (p j) -> f j p", j=NT)
            for g, js in groups:
                for j in js:
                    o = ps[:, g, (j - js[0]) * F:(j - js[0] + 1) * F]
                    nc.tensor.matmul(o, xT_v[:, j, :], wn1x[:, :], start=True, stop=False)
                    last = nc.tensor.matmul(o, ones_row[:, :], bn1r[:, :], start=False, stop=True)
                last.then_inc(xw_ready, 1)
            pe.wait_ge(w_in, 11 * 16)
            pe.wait_ge(xw_copied, len(groups))

            def front(turn, u):
                k = turn * U + u
                c = k + LEAD
                if not isinstance(c, int) or c < NCH:
                    s, t = (u + LEAD) % U, turn + (u + LEAD) // U
                    if s % 2 == 0:
                        pe.wait_ge(ea_in[s // 2], (t + 1) * 16)
                    wait_count(pe, h1_ready, c - 1)
                    rows = slice(EF * (s % 2), EF * (s % 2) + EF)
                    nc.tensor.matmul(ps_a[:, s % 2, :], we1[rows, :], ea[rows, s // 2, :], start=True, stop=True
                                     ).then_inc(a_ready, 1)
                c = k + 2
                if not isinstance(c, int) or 0 <= c < NCH:
                    pe.wait_ge(h1_ready, c + 1)
                    wait_count(pe, ef_ready, c - 1)
                    nc.tensor.matmul(ps_b[:, u % 2, :], we2[:, :], h1[:, u % 2, :], start=True, stop=True
                                     ).then_inc(b_ready, 1)
                c = k + 1
                if not isinstance(c, int) or 0 <= c < NCH:
                    b = (u + 1) % 2
                    pe.wait_ge(ef_ready, c + 1)
                    wait_count(pe, pre_ready, c - 1)
                    for t in range(tiles_of(c)):
                        last = nc.tensor.matmul(ps_c[:, b, t * F:(t + 1) * F], ef[:, b, t * P:(t + 1) * P],
                                                wn1e[:, :], start=True, stop=True)
                    last.then_inc(c_ready, 1)

            def narrow(turn, u):
                front(turn, u)
                k = turn * U + u
                if isinstance(k, int) and k < 0:
                    return
                b, tiles = u % 2, tiles_of(k)
                pe.wait_ge(r_ready, k + 1)
                pe.wait_ge(hot_ready, k + 1)
                wait_count(pe, acc_done, k - 1)
                for t in range(tiles):
                    nc.tensor.matmul(ps_d[:, b, 0:W], r[:, b, t * F:(t + 1) * F], hot[:, b, t, :],
                                     start=(t == 0), stop=(t == tiles - 1))
                for t in range(tiles):
                    hot_bf = hot[:, b, t, :].bitcast(BF16)[:, 1::2]
                    last = nc.tensor.matmul(ps_d[:, b, W:2 * W], ones_bf[:, :], hot_bf,
                                            start=(t == 0), stop=(t == tiles - 1))
                last.then_inc(d_ready, 1)

            def general(turn, u):
                front(turn, u)
                k = turn * U + u
                if isinstance(k, int) and k < 0:
                    return
                b, tiles = u % 2, tiles_of(k)
                with pe.Fori(0, NW) as w:
                    pe.wait_ge(r_ready, k + 1)
                    pe.wait_ge(wide_added, k * NW + w + 1)
                    for t in range(tiles):
                        pe.wait_ge(wide_ready, (k * NW) * TPC + w * tiles + t + 1)
                        nc.tensor.matmul(ps_d[:, 0, 0:WW], r[:, b, t * F:(t + 1) * F], hot_wide[:, t % 2, :],
                                         start=(t == 0), stop=(t == tiles - 1))
                        hot_bf = hot_wide[:, t % 2, :].bitcast(BF16)[:, 1::2]
                        last = nc.tensor.matmul(ps_d[:, 1, 0:WW], ones_bf[:, :], hot_bf,
                                                start=(t == 0), stop=(t == tiles - 1))
                        last.then_inc(wide_used, 1)
                    nc.tensor.drain().then_inc(wide_sum, 1)
                nc.tensor.drain().then_inc(d_ready, 1)

            pe.wait_ge(flag_ready, 1)
            is_narrow = nc.tensor.value_load(narrow_i[0:1, 0:1], min_val=0, max_val=1)
            with pe.If(is_narrow):
                main_steps(pe, narrow)
            with pe.Else():
                main_steps(pe, general)
            pe.wait_ge(acc_done, NCH)
            sums = acc[:, 0, :].rearrange("f (p j) -> f j p", j=NT)
            count = acc[0:1, 1, :].rearrange("f (p j) -> f j p", j=NT)
            for g, js in groups:
                for j in js:
                    o = ps[:, g, (j - js[0]) * F:(j - js[0] + 1) * F]
                    nc.tensor.matmul(o, sums[:, j, :], wn2[:, :], start=True, stop=False)
                    last = nc.tensor.matmul(o, count[:, j, :], bn2r[:, :], start=False, stop=True)
                last.then_inc(msg_ready, 1)

        @block.vector
        def _(dve):
            nc.vector.memset(ones_row[:, :], 1.0).then_inc(consts, 1)
            nc.vector.memset(ones_bf[:, :], 1.0).then_inc(consts, 1)
            nc.vector.memset(eps[:, :], EPS).then_inc(dve_prep, 1)
            dve.wait_ge(dst_in, 32)
            nc.vector.tensor_reduce(lo_c[:, :], dst_ci[:, :, :], axis=AXX, op=ALU.min).then_inc(span_ready, 1)
            nc.vector.tensor_reduce(hi_c[:, :], dst_ci[:, :, :], axis=AXX, op=ALU.max).then_inc(span_ready, 1)
            nc.vector.tensor_copy(dst_f[:, :], dst_i[:, :]).then_inc(dve_prep, 1)
            dve.wait_ge(iota_done, 1)
            nc.vector.tensor_copy(iota_f[:, :], iota_i[:, :]).then_inc(dve_prep, 1)
            dve.wait_ge(span_in, 32)
            nc.vector.tensor_tensor(span[:, :], hi_b[:, :], lo_b[:, :], ALU.subtract).then_inc(dve_prep, 1)
            nc.vector.tensor_copy(base_i[:, :], lo_b[:, :]).then_inc(dve_prep, 1)
            dve.wait_ge(dve_prep, 5)
            nc.vector.tensor_reduce(widest[:, :], span[:, :], axis=AXX, op=ALU.max).then_inc(dve_prep, 1)
            nc.vector.tensor_tensor(dst_rel[:, :].rearrange("p (c t) -> p c t", t=TPC),
                                    dst_f[:, :].rearrange("p (c t) -> p c t", t=TPC),
                                    lo_b[:, :].unsqueeze(2).broadcast_to([P, NCH, TPC]), ALU.subtract
                                    ).then_inc(dve_prep, 1)
            dve.wait_ge(dve_prep, 7)
            nc.vector.tensor_scalar(narrow_i[:, :], widest[:, :], float(W), None, ALU.is_lt
                                    ).then_inc(flag_ready, 1)
            dve.wait_ge(w_in, 11 * 16)
            dve.wait_ge(acc_zero, 1)
            dve.wait_ge(flag_ready, 1)

            def gate(turn, u):
                c = turn * U + u + 2
                if not isinstance(c, int) or 0 <= c < NCH:
                    b = u % 2
                    dve.wait_ge(b_ready, c + 1)
                    dve.wait_ge(tw_ready, c + 1)
                    wait_count(dve, c_ready, c - 1)
                    nc.vector.scalar_tensor_tensor(ef[:, b, :], ps_b[:, b, :], be2c[:, 0:1], tw[:, b, :],
                                                   op0=ALU.add, op1=ALU.mult).then_inc(ef_ready, 1)

            def add_gathered(turn, u):
                c = turn * U + u + 1
                if not isinstance(c, int) or 0 <= c < NCH:
                    s, t, tiles = (u + 1) % U, turn + (u + 1) // U, tiles_of(c)
                    dve.wait_ge(c_ready, c + 1)
                    dve.wait_ge(gath_in[s], t * (16 * TPC) + 16 * tiles)
                    wait_count(dve, r_ready, c - 1)
                    nc.vector.tensor_tensor(pre[:, s % 2, 0:tiles * F], ps_c[:, s % 2, 0:tiles * F],
                                            gath[:, s, 0:tiles * F], ALU.add).then_inc(pre_ready, 1)

            def narrow_step(turn, u, base):
                gate(turn, u)
                c = turn * U + u + 1
                if not isinstance(c, int) or 0 <= c < NCH:
                    b = (u + 1) % 2
                    wait_count(dve, d_ready, c - 1)
                    nc.vector.tensor_tensor(
                        hot[:, b, :, :], iota_f[:, 0:W].unsqueeze(1).broadcast_to([P, TPC, W]),
                        dst_rel[:, bass.ds(c * TPC, TPC)].unsqueeze(2).broadcast_to([P, TPC, W]),
                        ALU.is_equal).then_inc(hot_ready, 1)
                add_gathered(turn, u)
                k = turn * U + u
                if not isinstance(k, int) or k >= 0:
                    dve.wait_ge(d_ready, k + 1)
                    wait_count(dve, acc_done, k)
                    window = acc[:, :, bass.ds(base, W)]
                    nc.vector.tensor_tensor(window, window,
                                            ps_d[:, u % 2, 0:2 * W].rearrange("p (a w) -> p a w", a=2),
                                            ALU.add).then_inc(acc_done, 1)

            def bases(first, n):
                return nc.values_load_multi_w_load_instructions(
                    base_i[0:1, bass.ds(first, n)], engines=[mybir.EngineType.DVE],
                    min_val=0, max_val=NPAD - W, skip_runtime_bounds_check_because="a destination is a node or the padding value")[1]

            def general_step(turn, u):
                gate(turn, u)
                add_gathered(turn, u)
                k = turn * U + u
                if isinstance(k, int) and k < 0:
                    return
                tiles = tiles_of(k)
                with dve.Fori(0, NW) as w:
                    for t in range(tiles):
                        dve.wait_ge(wide_used, (k * NW) * TPC + w * tiles + t + 1)
                        at = k * TPC + t
                        nc.vector.tensor_scalar(hot_wide[:, t % 2, :], iota_f[:, bass.ds(w * WW, WW)],
                                                dst_f[:, bass.ds(at, 1)], None, ALU.is_equal
                                                ).then_inc(wide_ready, 1)
                    dve.wait_ge(wide_sum, k * NW + w + 1)
                    window = acc[:, :, bass.ds(w * WW, WW)]
                    nc.vector.tensor_tensor(window, window, ps_d[:, :, 0:WW], ALU.add).then_inc(wide_added, 1)
                nc.vector.drain().then_inc(acc_done, 1)

            is_narrow = nc.vector.value_load(narrow_i[0:1, 0:1], min_val=0, max_val=1)
            with dve.If(is_narrow):
                for k in range(-LEAD, U):
                    narrow_step(k // U, k % U, bases(k, 1)[0] if k >= 0 else None)
                with dve.Fori(1, TURNS) as turn:
                    at = bases(turn * U, U)
                    for u in range(U):
                        narrow_step(turn, u, at[u])
                for k in range(TURNS * U, NCH):
                    narrow_step(k // U, k % U, bases(k, 1)[0])
            with dve.Else():
                nc.vector.drain().then_inc(wide_used, 2)
                nc.vector.drain().then_inc(wide_added, 1)
                main_steps(dve, general_step)

            def normalise(g, js):
                dve.wait_ge(std_ready, g + 1)
                nc.vector.reciprocal(rstd[:, js[0]:js[-1] + 1], std[:, js[0]:js[-1] + 1]).then_inc(y_ready, 1)
                dve.wait_ge(y_ready, 2 * g + 2 + (g + 1 < len(groups)))
                for j in js:
                    at = y[:, j * F:(j + 1) * F]
                    nc.vector.tensor_scalar(at, at, mv[:, j, 0:1], rstd[:, j:j + 1], ALU.subtract, ALU.mult
                                            ).then_inc(norm_ready, 1)

            for g, js in groups:
                dve.wait_ge(msg_ready, g + 1)
                nc.vector.scalar_tensor_tensor(y[:, group_cols(js)], x_sb[:, group_cols(js)], 2.0,
                                               ps[:, g, 0:len(js) * F], op0=ALU.mult, op1=ALU.add
                                               ).then_inc(y_ready, 1)
                dve.wait_ge(y_ready, max(1, 2 * g))
                if g == 0:
                    dve.wait_ge(y_ready, 1)
                else:
                    dve.wait_ge(y_ready, 2 * g)
                for j in js:
                    nc.vector.bn_stats(stats[:, j, :], y[:, j * F:(j + 1) * F]).then_inc(dve_prep, 1)
                dve.wait_ge(dve_prep, 7 + js[-1] + 1)
                for j in js:
                    nc.vector.bn_aggr(mv[:, j, :], stats[:, j, :]).then_inc(mv_ready, 1)
                if g:
                    normalise(g - 1, groups[g - 1][1])
            normalise(*groups[-1])


def kernel(x, src, dst, edge_attr_64, edge_weight, L0_gnn_We1, L0_gnn_be1, L0_gnn_We2, L0_gnn_be2, L0_gnn_Wt,
           L0_gnn_bt, L0_gnn_Wn1, L0_gnn_bn1, L0_gnn_Wn2, L0_gnn_bn2):
    import concourse.bacc as bacc
    from concourse.bass_utils import run_bass_kernel_spmd

    def padded(a, rows, value=0):
        a = np.asarray(a)
        whole = np.full((rows,) + a.shape[1:], value, a.dtype)
        whole[:a.shape[0]] = a
        return whole

    xp = padded(x, NPAD)
    dp = padded(dst, EPAD, N_NODES)
    ep = padded(edge_attr_64, EPAD).reshape(NCH // 2, 2, C, EF)
    host = {
        "x": xp,
        "xT": xp.T,
        "src": padded(src, EPAD).reshape(NCH * TPC, P).T,
        "dst": dp.reshape(NCH * TPC, P).T,
        "dst_rows": dp.reshape(NCH // 2, 2, C),
        "edge_attr": ep.transpose(1, 3, 0, 2).reshape(2 * EF, NCH // 2 * C),
        "edge_weight": padded(edge_weight, EPAD).reshape(1, EPAD),
        "We1": L0_gnn_We1, "be1": L0_gnn_be1, "We2": L0_gnn_We2, "be2": L0_gnn_be2, "Wt": L0_gnn_Wt,
        "bt": L0_gnn_bt, "Wn1": L0_gnn_Wn1, "bn1": L0_gnn_bn1, "Wn2": L0_gnn_Wn2, "bn2": L0_gnn_bn2,
    }
    nc = bacc.Bacc("TRN2", target_bir_lowering=False, num_devices=1)
    arrays, args = {}, []
    for name, a in host.items():
        a = np.ascontiguousarray(a)
        arrays[f"in_{name}"] = a
        args.append(nc.dram_tensor(f"in_{name}", a.shape, mybir.dt.from_np(a.dtype), kind="ExternalInput").ap())
    args.append(nc.dram_tensor("out_y", (NPAD, F), F32, kind="ExternalOutput").ap())
    gnn_kernel(nc, *args)
    result = run_bass_kernel_spmd(nc, [arrays], core_ids=[0])
    return result.results[0]["out_y"][:N_NODES]
```

```python
import numpy as np

import concourse.bass as bass
from concourse import mybir
from contextlib import ExitStack

F32 = mybir.dt.float32
BF16 = mybir.dt.bfloat16
I32 = mybir.dt.int32
ALU = mybir.AluOpType
ACT = mybir.ActivationFunctionType
AXX = mybir.AxisListType.X

P = 128
N_NODES = 3125
N_EDGES = 103125
F = 128
EF = 64
NT = 25
NPAD = P * NT
TPC = 4
C = TPC * P
NCH = -(-N_EDGES // (2 * C)) * 2
NTILES = -(-N_EDGES // P)
EPAD = NCH * C
U = 8
IDX_LEAD = 2
IDX_RING = U // 2
EA_RING = 2
EW_RING = 4
W = 32
WW = 448
NW = -(-(N_NODES + 1) // WW)
EPS = 1e-5
LEAD = 3
COUNT_GAIN = 4
COUNT_LEAD = LEAD + COUNT_GAIN
TURNS = (NCH - COUNT_LEAD - 1) // U
RAW = 4


def tiles_of(c):
    return min(TPC, NTILES - c * TPC) if isinstance(c, int) else TPC


def wait_count(eng, sem, value):
    if not isinstance(value, int) or value > 0:
        eng.wait_ge(sem, value)


def counted_at(k):
    if not isinstance(k, int):
        return [k + COUNT_LEAD]
    gained = min(max(k - (U - COUNT_GAIN), 0), COUNT_GAIN)
    n = 2 if U - COUNT_GAIN <= k < U else 1
    return [c for c in range(k + LEAD + gained, k + LEAD + gained + n) if c < NCH]


def main_steps(eng, step):
    for k in range(-LEAD, U):
        step(k // U, k % U)
    with eng.Fori(1, TURNS) as turn:
        for u in range(U):
            step(turn, u)
    for k in range(TURNS * U, NCH):
        step(k // U, k % U)


def gnn_kernel(nc, x, xT, src, dst, dst_rows, edge_attr, edge_weight, Wn1x, weights_in,
               columns, rows, out):
    table = nc.dram_tensor("table", [NPAD, F], F32, kind="Internal").ap()
    degree_dram = nc.dram_tensor("degree_dram", [1, NPAD], F32, kind="Internal").ap()
    span_dram = nc.dram_tensor("span_dram", [2, NCH], F32, kind="Internal").ap()

    with ExitStack() as ctx:
        def sb(name, shape, dt=F32):
            return ctx.enter_context(nc.sbuf_tensor(name, shape, dt))

        def sem(name):
            return ctx.enter_context(nc.semaphore(name))

        wn1x = sb("wn1x", [P, F])
        weights = sb("weights", [P, 4, F])
        we1, we2, wn1e, wn2 = (weights[:, n, :] for n in range(4))
        cols = sb("cols", [P, 4])
        be1c, be2c, wtc, btc = (cols[:, n:n + 1] for n in range(4))
        wide_rows = sb("wide_rows", [P, 2 * F])
        bn1b, bn2b = wide_rows[:, 0:F], wide_rows[:, F:2 * F]
        ident = sb("ident", [P, P])
        xgT = sb("xgT", [P, RAW, C])
        ones_bf = sb("ones_bf", [P, P], BF16)
        xT_sb = sb("xT_sb", [P, NT, P])
        x_sb = sb("x_sb", [P, NT * F])
        xw = sb("xw", [P, NT * F])
        y = sb("y", [P, NT * F])
        dst_i = sb("dst_i", [P, NCH * TPC], I32)
        dst_f = sb("dst_f", [P, NCH * TPC])
        dst_rel = sb("dst_rel", [P, NCH * TPC])
        dst_ci = sb("dst_ci", [NCH // 2, 2, C], I32)
        lo_c = sb("lo_c", [NCH // 2, 2])
        hi_c = sb("hi_c", [NCH // 2, 2])
        lo_b = sb("lo_b", [P, NCH])
        hi_b = sb("hi_b", [P, NCH])
        span = sb("span", [P, NCH])
        base_i = sb("base_i", [P, NCH], I32)
        widest = sb("widest", [P, 1])
        narrow_i = sb("narrow_i", [P, 1], I32)
        iota_i = sb("iota_i", [P, WW], I32)
        iota_f = sb("iota_f", [P, WW])
        window_i = sb("window_i", [P, NW], I32)
        window_f = sb("window_f", [P, NW])
        idx = sb("idx", [P, IDX_RING, 2 * TPC], I32)
        ea = sb("ea", [P, EA_RING, C])
        ew = sb("ew", [P, EW_RING, C])
        gath = sb("gath", [P, U, C])
        h1 = sb("h1", [P, 2, C])
        tw = sb("tw", [P, 2, C])
        ef = sb("ef", [P, 2, C])
        pre = sb("pre", [P, 2, C])
        r = sb("r", [P, 2, C])
        hot = sb("hot", [P, 2, TPC, W])
        hot_count = sb("hot_count", [P, 2, TPC, W], BF16)
        hot_wide = sb("hot_wide", [P, 2, WW])
        acc = sb("acc", [P, NPAD])
        degree = sb("degree", [P, NPAD])
        degree_n = sb("degree_n", [P, NT])
        ysum = sb("ysum", [P, NT])
        nmean = sb("nmean", [P, NT])
        square = sb("square", [P, F])
        ssq = sb("ssq", [P, NT])
        std = sb("std", [P, NT])
        rstd = sb("rstd", [P, NT])
        eps = sb("eps", [P, 1])

        ps = ctx.enter_context(nc.psum_tensor("ps", [P, 8, 512], F32))
        ps_a, ps_n = ps[:, 0, :], ps[:, 1, :]
        ps_b, ps_c, ps_d = (ps[:, 2 * n:2 * n + 2, :] for n in range(1, 4))

        w_in = sem("w_in")
        xT_in = [sem(f"xT_in{n}") for n in range(4)]
        wn1_in = sem("wn1_in")
        x2_ready = sem("x2_ready")
        late_in = sem("late_in")
        rows_in = sem("rows_in")
        ident_zero = sem("ident_zero")
        ident_ready = sem("ident_ready")
        xg_ready = sem("xg_ready")
        xg_copied = sem("xg_copied")
        dst_in = [sem("dst_rows_in"), sem("dst_tiles_in")]
        consts = sem("consts")
        iota_done = sem("iota_done")
        acc_zero = sem("acc_zero")
        xw_ready = sem("xw_ready")
        xw_copied = sem("xw_copied")
        table_out = sem("table_out")
        span_ready = sem("span_ready")
        span_out = sem("span_out")
        span_in = sem("span_in")
        dve_prep = sem("dve_prep")
        flag_ready = sem("flag_ready")
        idx_in = [sem(f"idx_in{n}") for n in range(IDX_RING)]
        ea_in = [sem(f"ea_in{n}") for n in range(EA_RING)]
        ew_in = [sem(f"ew_in{n}") for n in range(EW_RING)]
        gath_in = [sem(f"gath_in{n}") for n in range(U)]
        tables_ready = sem("tables_ready")
        slots_granted = sem("slots_granted")
        a_ready = sem("a_ready")
        h1_ready = sem("h1_ready")
        b_ready = sem("b_ready")
        tw_ready = sem("tw_ready")
        ef_ready = sem("ef_ready")
        c_ready = sem("c_ready")
        pre_ready = sem("pre_ready")
        r_ready = sem("r_ready")
        hot_ready = sem("hot_ready")
        d_ready = sem("d_ready")
        hot_count_ready = sem("hot_count_ready")
        count_ready = sem("count_ready")
        count_added = sem("count_added")
        degree_out = sem("degree_out")
        degree_in = sem("degree_in")
        acc_done = sem("acc_done")
        wide_ready = sem("wide_ready")
        wide_used = sem("wide_used")
        wide_sum = sem("wide_sum")
        wide_added = sem("wide_added")
        msg_ready = sem("msg_ready")
        y0_ready = sem("y0_ready")
        y_ready = sem("y_ready")
        nmean_ready = sem("nmean_ready")
        ssq_ready = sem("ssq_ready")
        std_ready = sem("std_ready")
        rstd_ready = sem("rstd_ready")
        norm_ready = [sem(f"norm_ready{g}") for g in range(-(-NT // 4))]
        out_done = sem("out_done")

        block = ctx.enter_context(nc.Block())

        src_v = src.rearrange("p (n t) -> p n t", t=2 * TPC)
        ea_v = edge_attr.rearrange("p (n c) -> p n c", c=C)
        x_rows = x.rearrange("(p j) f -> p (j f)", j=NT)
        out_rows = out.rearrange("(p j) f -> p (j f)", j=NT)
        table_rows = table.rearrange("(p j) f -> p (j f)", j=NT)
        groups = [(g, range(g * 4, min(g * 4 + 4, NT))) for g in range(-(-NT // 4))]

        xT_parts = [(0, 4), (4, 12), (12, 20), (20, NT)]

        def group_cols(js):
            return slice(js[0] * F, (js[-1] + 1) * F)

        def normalise(engine, j):
            at = y[:, j * F:(j + 1) * F]
            return engine.tensor_scalar(at, at, nmean[:, j:j + 1], rstd[:, j:j + 1], ALU.add, ALU.mult)

        @block.sync
        def _(sp):
            sp.dma_start(idx[:, 0, :], src_v[:, 0, :]).then_inc(idx_in[0], 16)
            sp.dma_start(wn1x[:, :], Wn1x).then_inc(wn1_in, 16)
            for n, (a, b) in enumerate(xT_parts):
                sp.dma_start(xT_sb[:, a:b, :], xT[:, a * P:b * P].rearrange("f (j p) -> f j p", p=P)
                             ).then_inc(xT_in[n], 16)
                if n == 0:
                    sp.dma_start(dst_ci[:, :, :], dst_rows).then_inc(dst_in[0], 16)
                if n == 1:
                    sp.dma_start(idx[:, 1, :], src_v[:, 1, :]).then_inc(idx_in[1], 16)
            sp.dma_start(dst_i[:, :], dst).then_inc(dst_in[1], 16)
            sp.wait_ge(span_ready, 2)
            for n, part in enumerate((lo_c, hi_c)):
                sp.dma_start(span_dram[n, :].rearrange("(p a) -> p a", a=2), part[:, :]).then_inc(span_out, 16)
            sp.wait_ge(span_out, 32)
            for n, part in enumerate((lo_b, hi_b)):
                sp.dma_start(part[:, :], span_dram[n:n + 1, :].partition_broadcast(P)).then_inc(span_in, 16)
            sp.wait_ge(xw_copied, len(groups))

            def load_indices(turn, q):
                pair = turn * IDX_RING + q
                if not isinstance(turn, int) or turn:
                    for slot in (2 * q, 2 * q + 1):
                        sp.wait_ge(gath_in[slot], turn * (16 * TPC))
                sp.dma_start(idx[:, q, :], src_v[:, bass.ds(pair, 1), :]).then_inc(idx_in[q], 16)

            def load_pair(pair, slot):
                wait_count(sp, a_ready, 2 * (pair - EA_RING) + 2)
                sp.dma_start(ea[:, slot, :], ea_v[:, bass.ds(pair, 1), :]).then_inc(ea_in[slot], 16)
                for n in range(2):
                    c = pair * 2 + n
                    wait_count(sp, tw_ready, c - EW_RING + 1)
                    sp.dma_start(ew[:, 2 * slot + n, :], edge_weight[:, bass.ds(c * C, C)].partition_broadcast(P)
                                 ).then_inc(ew_in[2 * slot + n], 16)

            load_pair(0, 0)
            load_indices(0, 2)
            sp.wait_ge(table_out, 16 * len(groups))
            load_indices(0, 3)
            load_pair(1, 1)
            load_indices(1, 0)
            load_pair(2, 0)
            load_indices(1, 1)
            load_pair(3, 1)
            with sp.Fori(1, NCH // U - 1) as turn:
                for q in range(IDX_RING):
                    load_indices(turn + (q + IDX_LEAD) // IDX_RING, (q + IDX_LEAD) % IDX_RING)
                    load_pair(turn * IDX_RING + q, q % EA_RING)
            for pair in range((NCH // U - 1) * IDX_RING, NCH // 2):
                if pair + IDX_LEAD < NCH // 2:
                    load_indices((pair + IDX_LEAD) // IDX_RING, (pair + IDX_LEAD) % IDX_RING)
                load_pair(pair, pair % EA_RING)
            for g, js in groups:
                sp.wait_ge(norm_ready[g], len(js))
                sp.dma_start(out_rows[:, group_cols(js)], y[:, group_cols(js)]).then_inc(out_done, 16)
            sp.wait_ge(out_done, 16 * len(groups))

        @block.gpsimd
        def _(pool):
            nc.gpsimd.memset(ident[:, :], 0.0).then_inc(ident_zero, 1)
            pool.wait_ge(ident_zero, 1)
            nc.gpsimd.affine_select(out=ident[:, :], in_=ident[:, :], compare_op=ALU.not_equal, fill=1.0,
                                    base=0, pattern=[[-1, P]], channel_multiplier=1).then_inc(ident_ready, 1)
            nc.gpsimd.iota(iota_i[:, :], pattern=[[1, WW]], base=0, channel_multiplier=0).then_inc(iota_done, 1)
            nc.gpsimd.iota(window_i[:, :], pattern=[[WW, NW]], base=0, channel_multiplier=0).then_inc(iota_done, 1)

            def gather(turn, u):
                c = turn * U + u
                if u % 2 == 0:
                    pool.wait_ge(idx_in[u // 2], (turn + 1) * 16)
                if isinstance(c, int) and U <= c < U + RAW:
                    pool.wait_ge(xg_ready, c - U + 1)
                else:
                    wait_count(pool, pre_ready, c - U + 1)
                pool.sem_inc(slots_granted, 1)
                tiles = tiles_of(c)
                for t in range(tiles):
                    at = TPC * (u % 2) + t
                    pool.indirect_dma_start(
                        gath[:, u, t * F:(t + 1) * F], None, x if isinstance(c, int) and c < RAW else table,
                        bass.IndirectOffsetOnAxis(idx[:, u // 2, at:at + 1], 0)).then_inc(gath_in[u], 16)

            for c in range(U + RAW):
                if c == RAW:
                    nc.gpsimd.memset(acc[:, :], 0.0).then_inc(acc_zero, 1)
                    pool.wait_ge(table_out, 16 * len(groups))
                gather(c // U, c % U)
            with pool.Fori(1, NCH // U - 1) as turn:
                for u in range(RAW, U + RAW):
                    gather(turn + u // U, u % U)
            for c in range((NCH // U - 1) * U + RAW, NCH):
                gather(c // U, c % U)
            for g, js in groups:
                pool.wait_ge(rstd_ready, g + 1)
                for j in js[1:]:
                    normalise(nc.gpsimd, j).then_inc(norm_ready[g], 1)

        @block.scalar
        def _(act):
            act.wait_ge(consts, 2)
            nc.scalar.activation(std[:, 0:1], eps[:, :], ACT.Sigmoid).then_inc(tables_ready, 1)
            act.dma_start(wide_rows[:, :], rows.rearrange("(a n) -> a n", a=1).partition_broadcast(P)
                          ).then_inc(rows_in, 16)
            act.wait_ge(xT_in[0], 16)
            act.dma_start(weights[:, :, :], weights_in).then_inc(w_in, 16)
            act.dma_start(cols[:, :], columns).then_inc(w_in, 16)
            for g, js in groups:
                act.wait_ge(xw_copied, g + 1)
                act.dma_start(table_rows[:, group_cols(js)], xw[:, group_cols(js)]).then_inc(table_out, 16)
            for c in range(RAW):
                act.wait_ge(xg_ready, c + 1)
                nc.scalar.activation(xgT[:, c, :], ps[:, (7 + c) % 8, :], ACT.Copy).then_inc(xg_copied, 1)
            act.wait_ge(w_in, 32)

            act.wait_ge(flag_ready, 1)
            is_narrow = nc.scalar.value_load(narrow_i[0:1, 0:1], min_val=0, max_val=1)

            def degrees_out():
                act.wait_ge(count_added, NCH)
                act.dma_start(degree_dram, degree[0:1, :]).then_inc(degree_out, 16)

            def degrees_in():
                act.wait_ge(degree_out, 16)
                act.dma_start(degree_n[:, :], degree_dram.rearrange("a (p j) -> (a p) j", j=NT)
                              ).then_inc(degree_in, 16)

            def step(turn, u):
                k = turn * U + u
                if isinstance(k, int) and k in (NCH - COUNT_LEAD, NCH - COUNT_LEAD + 1):
                    with act.If(is_narrow):
                        degrees_out() if k == NCH - COUNT_LEAD else degrees_in()
                if isinstance(k, int) and k == U - 1:
                    act.dma_start(x_sb[:, :], x_rows).then_inc(late_in, 16)
                if isinstance(k, int) and k == TURNS * U:
                    act.wait_ge(late_in, 16)
                    nc.scalar.activation(x_sb[:, :], x_sb[:, :], ACT.Copy, scale=2.0).then_inc(x2_ready, 1)
                if not isinstance(k, int) or k >= 0:
                    act.wait_ge(pre_ready, k + 1)
                    wait_count(act, d_ready, k - 1)
                    n = tiles_of(k) * F
                    nc.scalar.activation(r[:, u % 2, 0:n], pre[:, u % 2, 0:n], ACT.Relu).then_inc(r_ready, 1)
                c = k + 3
                if not isinstance(c, int) or 0 <= c < NCH:
                    s = (u + 3) % EW_RING
                    act.wait_ge(ew_in[s], (turn * (U // EW_RING) + (u + 3) // EW_RING + 1) * 16)
                    wait_count(act, ef_ready, c - 1)
                    nc.scalar.activation(tw[:, s % 2, :], ew[:, s, :], ACT.Sigmoid, bias=btc, scale=wtc
                                         ).then_inc(tw_ready, 1)
                    act.wait_ge(a_ready, c + 1)
                    wait_count(act, b_ready, c - 1)
                    nc.scalar.activation(h1[:, s % 2, :], ps_a, ACT.Relu, bias=be1c
                                         ).then_inc(h1_ready, 1)

            main_steps(act, step)
            with act.If(is_narrow):
                pass
            with act.Else():
                degrees_out()
                degrees_in()
            nc.scalar.activation(std[:, 1:2], eps[:, :], ACT.Sqrt).then_inc(tables_ready, 1)
            act.wait_ge(tables_ready, 2)
            for g, js in groups:
                act.wait_ge(nmean_ready, g + 1)
                for j in js:
                    act.wait_ge(ssq_ready, j) if j else None
                    nc.scalar.activation(square[:, :], y[:, j * F:(j + 1) * F], ACT.Square,
                                         bias=nmean[:, j:j + 1], accum_out=ssq[:, j:j + 1]).then_inc(ssq_ready, 1)
                act.wait_ge(ssq_ready, js[-1] + 1)
                nc.scalar.activation(std[:, js[0]:js[-1] + 1], ssq[:, js[0]:js[-1] + 1], ACT.Sqrt,
                                     bias=eps[:, 0:1], scale=1.0 / F).then_inc(std_ready, 1)

        @block.tensor
        def _(pe):
            pe.wait_ge(wn1_in, 16)
            for g, js in groups:
                for j in js:
                    o = ps[:, g, (j - js[0]) * F:(j - js[0] + 1) * F]
                    part = [a for a, _ in xT_parts].index(j) if j in [a for a, _ in xT_parts] else None
                    if part is not None:
                        pe.wait_ge(xT_in[part], 16)
                    last = nc.tensor.matmul(o, xT_sb[:, j, :], wn1x[:, :], start=True, stop=True)
                last.then_inc(xw_ready, 1)
            pe.wait_ge(ident_ready, 1)
            for c in range(RAW):
                pe.wait_ge(gath_in[c], 16 * TPC)
                wait_count(pe, xw_copied, c)
                for t in range(TPC):
                    last = nc.tensor.transpose(ps[:, (7 + c) % 8, t * P:(t + 1) * P],
                                               gath[:, c, t * F:(t + 1) * F], ident[:, :])
                last.then_inc(xg_ready, 1)
            pe.wait_ge(w_in, 32)
            pe.wait_ge(consts, 1)
            pe.wait_ge(xw_copied, len(groups))
            pe.wait_ge(xg_copied, RAW)

            def front(turn, u):
                k = turn * U + u
                c = k + 3
                if not isinstance(c, int) or 0 <= c < NCH:
                    s, pair = (u + 3) % 2, (u + 3) // 2
                    if s == 0:
                        pe.wait_ge(ea_in[pair % EA_RING], (turn * (IDX_RING // EA_RING) + pair // EA_RING + 1) * 16)
                    wait_count(pe, h1_ready, c)
                    rows = slice(EF * s, EF * s + EF)
                    nc.tensor.matmul(ps_a, we1[rows, :], ea[rows, pair % EA_RING, :], start=True, stop=True
                                     ).then_inc(a_ready, 1)
                c = k + 2
                if not isinstance(c, int) or 0 <= c < NCH:
                    pe.wait_ge(h1_ready, c + 1)
                    wait_count(pe, ef_ready, c - 1)
                    nc.tensor.matmul(ps_b[:, u % 2, :], we2, h1[:, u % 2, :], start=True, stop=True
                                     ).then_inc(b_ready, 1)
                c = k + 1
                if not isinstance(c, int) or 0 <= c < NCH:
                    b = (u + 1) % 2
                    pe.wait_ge(ef_ready, c + 1)
                    wait_count(pe, pre_ready, c - 1)
                    raw = isinstance(c, int) and c < RAW
                    for t in range(tiles_of(c)):
                        last = nc.tensor.matmul(ps_c[:, b, t * F:(t + 1) * F], ef[:, b, t * P:(t + 1) * P],
                                                wn1e, start=True, stop=not raw)
                        if raw:
                            last = nc.tensor.matmul(ps_c[:, b, t * F:(t + 1) * F], xgT[:, c, t * P:(t + 1) * P],
                                                    wn1x[:, :], start=False, stop=True)
                    last.then_inc(c_ready, 1)

            def narrow(turn, u):
                front(turn, u)
                k = turn * U + u
                for c in counted_at(k):
                    slot = c % 2 if isinstance(c, int) else (u + COUNT_LEAD) % 2
                    pe.wait_ge(hot_count_ready, c + 1)
                    wait_count(pe, count_added, c)
                    for t in range(tiles_of(c)):
                        last = nc.tensor.matmul(ps_n[:, 0:W], ones_bf[:, :], hot_count[:, slot, t, :],
                                                start=(t == 0), stop=(t == tiles_of(c) - 1))
                    last.then_inc(count_ready, 1)
                if isinstance(k, int) and k < 0:
                    return
                b, tiles = u % 2, tiles_of(k)
                pe.wait_ge(r_ready, k + 1)
                pe.wait_ge(hot_ready, k + 1)
                wait_count(pe, acc_done, k - 1)
                for t in range(tiles):
                    last = nc.tensor.matmul(ps_d[:, b, 0:W], r[:, b, t * F:(t + 1) * F], hot[:, b, t, :],
                                            start=(t == 0), stop=(t == tiles - 1))
                last.then_inc(d_ready, 1)

            def general(turn, u):
                front(turn, u)
                k = turn * U + u
                if isinstance(k, int) and k < 0:
                    return
                b, tiles = u % 2, tiles_of(k)
                with pe.Fori(0, NW) as w:
                    pe.wait_ge(r_ready, k + 1)
                    pe.wait_ge(wide_added, k * NW + w + 1)
                    for t in range(tiles):
                        pe.wait_ge(wide_ready, (k * NW) * TPC + w * tiles + t + 1)
                        nc.tensor.matmul(ps_d[:, 0, 0:WW], r[:, b, t * F:(t + 1) * F], hot_wide[:, t % 2, :],
                                         start=(t == 0), stop=(t == tiles - 1))
                        hot_bf = hot_wide[:, t % 2, :].bitcast(BF16)[:, 1::2]
                        last = nc.tensor.matmul(ps_d[:, 1, 0:WW], ones_bf[:, :], hot_bf,
                                                start=(t == 0), stop=(t == tiles - 1))
                        last.then_inc(wide_used, 1)
                    nc.tensor.drain().then_inc(wide_sum, 1)
                nc.tensor.drain().then_inc(d_ready, 1)

            pe.wait_ge(flag_ready, 1)
            is_narrow = nc.tensor.value_load(narrow_i[0:1, 0:1], min_val=0, max_val=1)
            with pe.If(is_narrow):
                main_steps(pe, narrow)
            with pe.Else():
                main_steps(pe, general)
            pe.wait_ge(acc_done, NCH)
            sums = acc[:, :].rearrange("f (p j) -> f j p", j=NT)
            for g, js in groups:
                for j in js:
                    last = nc.tensor.matmul(ps[:, g, (j - js[0]) * F:(j - js[0] + 1) * F], sums[:, j, :],
                                            wn2, start=True, stop=True)
                last.then_inc(msg_ready, 1)

        @block.vector
        def _(dve):
            def measure_spans():
                dve.wait_ge(dst_in[1], 16)
                nc.vector.tensor_copy(dst_f[:, :], dst_i[:, :]).then_inc(dve_prep, 1)
                dve.wait_ge(iota_done, 2)
                nc.vector.tensor_copy(iota_f[:, :], iota_i[:, :]).then_inc(dve_prep, 1)
                nc.vector.tensor_copy(window_f[:, :], window_i[:, :]).then_inc(dve_prep, 1)
                dve.wait_ge(span_in, 32)
                nc.vector.tensor_tensor(span[:, :], hi_b[:, :], lo_b[:, :], ALU.subtract).then_inc(dve_prep, 1)
                nc.vector.tensor_copy(base_i[:, :], lo_b[:, :]).then_inc(dve_prep, 1)
                dve.wait_ge(dve_prep, 5)
                nc.vector.tensor_reduce(widest[:, :], span[:, :], axis=AXX, op=ALU.max).then_inc(dve_prep, 1)
                nc.vector.tensor_tensor(dst_rel[:, :].rearrange("p (c t) -> p c t", t=TPC),
                                        dst_f[:, :].rearrange("p (c t) -> p c t", t=TPC),
                                        lo_b[:, :].unsqueeze(2).broadcast_to([P, NCH, TPC]), ALU.subtract
                                        ).then_inc(dve_prep, 1)
                dve.wait_ge(dve_prep, 7)
                nc.vector.tensor_scalar(narrow_i[:, :], widest[:, :], float(W), None, ALU.is_lt
                                        ).then_inc(flag_ready, 1)

            nc.vector.memset(ones_bf[:, :], 1.0).then_inc(consts, 1)
            nc.vector.memset(eps[:, :], EPS).then_inc(consts, 1)
            nc.vector.memset(degree[:, :], 0.0).then_inc(acc_zero, 1)
            dve.wait_ge(dst_in[0], 16)
            nc.vector.tensor_reduce(lo_c[:, :], dst_ci[:, :, :], axis=AXX, op=ALU.min).then_inc(span_ready, 1)
            nc.vector.tensor_reduce(hi_c[:, :], dst_ci[:, :, :], axis=AXX, op=ALU.max).then_inc(span_ready, 1)
            dve.wait_ge(rows_in, 16)
            for g, js in groups:
                dve.wait_ge(xw_ready, g + 1)
                nc.vector.tensor_tensor(
                    xw[:, group_cols(js)].rearrange("p (j f) -> p j f", f=F),
                    ps[:, g, 0:len(js) * F].rearrange("p (j f) -> p j f", f=F),
                    bn1b.unsqueeze(1).broadcast_to([P, len(js), F]), ALU.add).then_inc(xw_copied, 1)
            measure_spans()
            dve.wait_ge(w_in, 32)
            dve.wait_ge(acc_zero, 2)
            dve.wait_ge(flag_ready, 1)

            def gate(turn, u):
                c = turn * U + u + 2
                if not isinstance(c, int) or 0 <= c < NCH:
                    b = u % 2
                    dve.wait_ge(b_ready, c + 1)
                    dve.wait_ge(tw_ready, c + 1)
                    wait_count(dve, c_ready, c - 1)
                    nc.vector.scalar_tensor_tensor(ef[:, b, :], ps_b[:, b, :], be2c, tw[:, b, :],
                                                   op0=ALU.add, op1=ALU.mult).then_inc(ef_ready, 1)

            def add_gathered(turn, u):
                c = turn * U + u + 1
                if not isinstance(c, int) or 0 <= c < NCH:
                    s, t, tiles = (u + 1) % U, turn + (u + 1) // U, tiles_of(c)
                    dve.wait_ge(c_ready, c + 1)
                    wait_count(dve, r_ready, c - 1)
                    if isinstance(c, int) and c < RAW:
                        nc.vector.tensor_tensor(pre[:, s % 2, :].rearrange("p (t f) -> p t f", f=F),
                                                ps_c[:, s % 2, :].rearrange("p (t f) -> p t f", f=F),
                                                bn1b.unsqueeze(1).broadcast_to([P, TPC, F]), ALU.add
                                                ).then_inc(pre_ready, 1)
                        return
                    dve.wait_ge(gath_in[s], t * (16 * TPC) + 16 * tiles)
                    nc.vector.tensor_tensor(pre[:, s % 2, 0:tiles * F], ps_c[:, s % 2, 0:tiles * F],
                                            gath[:, s, 0:tiles * F], ALU.add).then_inc(pre_ready, 1)

            def add_degrees(js):
                dve.wait_ge(degree_in, 16)
                dve.wait_ge(x2_ready, 1)
                for j in js:
                    at = x_sb[:, j * F:(j + 1) * F]
                    nc.vector.scalar_tensor_tensor(at, bn2b, degree_n[:, j:j + 1], at, op0=ALU.mult,
                                                   op1=ALU.add).then_inc(y0_ready, 1)

            def one_hot(rows, c):
                return nc.vector.tensor_tensor(
                    rows, iota_f[:, 0:W].unsqueeze(1).broadcast_to([P, TPC, W]),
                    dst_rel[:, bass.ds(c * TPC, TPC)].unsqueeze(2).broadcast_to([P, TPC, W]), ALU.is_equal)

            def one_hot_count(c, slot):
                one_hot(hot_count[:, slot, :, :], c).then_inc(hot_count_ready, 1)

            def narrow_step(turn, u, base, count_bases):
                k = turn * U + u
                gate(turn, u)
                for c, count_base in zip(counted_at(k), count_bases):
                    dve.wait_ge(count_ready, c + 1)
                    wait_count(dve, count_added, c)
                    window = degree[:, bass.ds(count_base, W)]
                    nc.vector.tensor_tensor(window, window, ps_n[:, 0:W], ALU.add).then_inc(count_added, 1)
                for c in counted_at(k + 1):
                    one_hot_count(c, c % 2 if isinstance(c, int) else (u + 1 + COUNT_LEAD) % 2)
                c = k + 1
                if not isinstance(c, int) or 0 <= c < NCH:
                    wait_count(dve, d_ready, c - 1)
                    one_hot(hot[:, (u + 1) % 2, :, :], c).then_inc(hot_ready, 1)
                if isinstance(k, int) and k >= NCH - 6:
                    n = k - (NCH - 6)
                    add_degrees(range(n * NT // 5, min(NT, (n + 1) * NT // 5)))
                add_gathered(turn, u)
                if not isinstance(k, int) or k >= 0:
                    dve.wait_ge(d_ready, k + 1)
                    wait_count(dve, acc_done, k)
                    window = acc[:, bass.ds(base, W)]
                    nc.vector.tensor_tensor(window, window, ps_d[:, u % 2, 0:W], ALU.add).then_inc(acc_done, 1)

            def bases(first, n):
                return nc.values_load_multi_w_load_instructions(
                    base_i[0:1, bass.ds(first, n)], engines=[mybir.EngineType.DVE],
                    min_val=0, max_val=NPAD - W, skip_runtime_bounds_check_because="a destination is a node or the padding value")[1]

            def general_step(turn, u):
                gate(turn, u)
                add_gathered(turn, u)
                k = turn * U + u
                if isinstance(k, int) and k < 0:
                    return
                tiles = tiles_of(k)
                with dve.Fori(0, NW) as w:
                    for t in range(tiles):
                        dve.wait_ge(wide_used, (k * NW) * TPC + w * tiles + t + 1)
                        at = k * TPC + t
                        nc.vector.tensor_scalar(hot_wide[:, t % 2, :], iota_f[:, :], window_f[:, bass.ds(w, 1)],
                                                dst_f[:, bass.ds(at, 1)], ALU.add, ALU.is_equal
                                                ).then_inc(wide_ready, 1)
                    dve.wait_ge(wide_sum, k * NW + w + 1)
                    for n, total in enumerate((acc, degree)):
                        window = total[:, bass.ds(w * WW, WW)]
                        last = nc.vector.tensor_tensor(window, window, ps_d[:, n, 0:WW], ALU.add)
                    last.then_inc(wide_added, 1)
                nc.vector.drain().then_inc(acc_done, 1)
                nc.vector.drain().then_inc(count_added, 1)

            is_narrow = nc.vector.value_load(narrow_i[0:1, 0:1], min_val=0, max_val=1)
            with dve.If(is_narrow):
                for c in counted_at(-LEAD):
                    one_hot_count(c, c % 2)

                def peeled(k):
                    narrow_step(k // U, k % U, bases(k, 1)[0] if k >= 0 else None,
                                [bases(c, 1)[0] for c in counted_at(k)])

                for k in range(-LEAD, U):
                    peeled(k)
                with dve.Fori(1, TURNS) as turn:
                    at, count_at = bases(turn * U, U), bases(turn * U + COUNT_LEAD, U)
                    for u in range(U):
                        narrow_step(turn, u, at[u], [count_at[u]])
                for k in range(TURNS * U, NCH):
                    peeled(k)
            with dve.Else():
                nc.vector.drain().then_inc(wide_used, 2)
                nc.vector.drain().then_inc(wide_added, 1)
                main_steps(dve, general_step)
                add_degrees(range(NT))

            def finish(g, js):
                dve.wait_ge(std_ready, g + 1)
                nc.vector.reciprocal(rstd[:, js[0]:js[-1] + 1], std[:, js[0]:js[-1] + 1]).then_inc(rstd_ready, 1)
                dve.wait_ge(rstd_ready, g + 1)
                for j in js[:1]:
                    normalise(nc.vector, j).then_inc(norm_ready[g], 1)

            dve.wait_ge(y0_ready, NT)
            for g, js in groups:
                dve.wait_ge(msg_ready, g + 1)
                for j in js:
                    nc.vector.scalar_tensor_tensor(
                        y[:, j * F:(j + 1) * F], ps[:, g, (j - js[0]) * F:(j - js[0] + 1) * F], 1.0,
                        x_sb[:, j * F:(j + 1) * F], op0=ALU.mult, op1=ALU.add,
                        accum_out=ysum[:, j:j + 1]).then_inc(y_ready, 1)
                dve.wait_ge(y_ready, js[-1] + 1)
                nc.vector.tensor_scalar(nmean[:, js[0]:js[-1] + 1], ysum[:, js[0]:js[-1] + 1], -1.0 / F, None,
                                        ALU.mult).then_inc(nmean_ready, 1)
                if g:
                    finish(g - 1, groups[g - 1][1])
            finish(*groups[-1])


def kernel(x, src, dst, edge_attr_64, edge_weight, L0_gnn_We1, L0_gnn_be1, L0_gnn_We2, L0_gnn_be2, L0_gnn_Wt,
           L0_gnn_bt, L0_gnn_Wn1, L0_gnn_bn1, L0_gnn_Wn2, L0_gnn_bn2):
    import concourse.bacc as bacc
    from concourse.bass_utils import run_bass_kernel_spmd

    def padded(a, rows, value=0):
        a = np.asarray(a)
        whole = np.full((rows,) + a.shape[1:], value, a.dtype)
        whole[:a.shape[0]] = a
        return whole

    xp = padded(x, NPAD)
    dp = padded(dst, EPAD, N_NODES)
    ep = padded(edge_attr_64, EPAD).reshape(NCH // 2, 2, C, EF)
    host = {
        "x": xp,
        "xT": xp.reshape(P, NT, F).transpose(2, 1, 0).reshape(F, NPAD),
        "src": padded(src, EPAD).reshape(NCH * TPC, P).T,
        "dst": dp.reshape(NCH * TPC, P).T,
        "dst_rows": dp.reshape(NCH // 2, 2, C),
        "edge_attr": ep.transpose(1, 3, 0, 2).reshape(2 * EF, NCH // 2 * C),
        "edge_weight": padded(edge_weight, EPAD).reshape(1, EPAD),
        "Wn1x": np.asarray(L0_gnn_Wn1)[:F],
        "weights": np.stack([np.concatenate([L0_gnn_We1, L0_gnn_We1]), L0_gnn_We2, np.asarray(L0_gnn_Wn1)[F:],
                       L0_gnn_Wn2], axis=1),
        "columns": np.stack([L0_gnn_be1, L0_gnn_be2, np.asarray(L0_gnn_Wt)[0], L0_gnn_bt], axis=1),
        "rows": np.concatenate([L0_gnn_bn1, L0_gnn_bn2]),
    }
    nc = bacc.Bacc("TRN2", target_bir_lowering=False, num_devices=1)
    arrays, args = {}, []
    for name, a in host.items():
        a = np.ascontiguousarray(a)
        arrays[f"in_{name}"] = a
        args.append(nc.dram_tensor(f"in_{name}", a.shape, mybir.dt.from_np(a.dtype), kind="ExternalInput").ap())
    args.append(nc.dram_tensor("out_y", (NPAD, F), F32, kind="ExternalOutput").ap())
    gnn_kernel(nc, *args)
    result = run_bass_kernel_spmd(nc, [arrays], core_ids=[0])
    return result.results[0]["out_y"][:N_NODES]
```

```python
import numpy as np

import concourse.bass as bass
from concourse import mybir
from contextlib import ExitStack

F32 = mybir.dt.float32
BF16 = mybir.dt.bfloat16
I32 = mybir.dt.int32
ALU = mybir.AluOpType
ACT = mybir.ActivationFunctionType
AXX = mybir.AxisListType.X

P = 128
N_NODES = 3125
N_EDGES = 103125
F = 128
EF = 64
NT = 25
NPAD = P * NT
TPC = 4
C = TPC * P
NCH = -(-N_EDGES // (2 * C)) * 2
NTILES = -(-N_EDGES // P)
EPAD = NCH * C
U = 8
IDX_LEAD = 2
IDX_RING = U // 2
EA_RING = 2
EW_RING = 4
W = 32
WW = 448
NW = -(-(N_NODES + 1) // WW)
EPS = 1e-5
LEAD = 3
COUNT_GAIN = U
TURNS = (NCH - LEAD - 1) // U - 2
EARLY = 22
EARLY_CHUNKS = 16
RAW = 4


GROUPS = [range(j, min(j + 4, EARLY)) for j in range(0, EARLY, 4)] + [range(EARLY, NT)]
BATCHES = [range(EARLY), range(EARLY, NT)]
DVE_SOON = 1
POOL_TILES = 10
DVE_LATE = 3


def tiles_of(c):
    return min(TPC, NTILES - c * TPC) if isinstance(c, int) else TPC


def wait_count(eng, sem, value):
    if not isinstance(value, int) or value > 0:
        eng.wait_ge(sem, value)


def counted_at(k):
    if not isinstance(k, int):
        return [k + LEAD]
    gained = min(max(k - TURNS * U, 0), COUNT_GAIN)
    n = 2 if TURNS * U <= k < TURNS * U + COUNT_GAIN else 1
    return [c for c in range(k + LEAD + gained, k + LEAD + gained + n) if c < NCH]


def early_group(k):
    g = k - (NCH - EARLY_CHUNKS) if isinstance(k, int) else -1
    return GROUPS[g] if 0 <= g < len(GROUPS) - 1 else []


def main_steps(eng, step):
    for k in range(-LEAD, U):
        step(k // U, k % U)
    with eng.Fori(1, TURNS) as turn:
        for u in range(U):
            step(turn, u)
    for k in range(TURNS * U, NCH):
        step(k // U, k % U)


def gnn_kernel(nc, x, xT, src, dst, dst_rows, edge_attr, edge_weight, Wn1x, weights_in,
               columns, rows, out):
    table = nc.dram_tensor("table", [NPAD, F], F32, kind="Internal").ap()
    span_dram = nc.dram_tensor("span_dram", [2, NCH], F32, kind="Internal").ap()

    with ExitStack() as ctx:
        def sb(name, shape, dt=F32):
            return ctx.enter_context(nc.sbuf_tensor(name, shape, dt))

        def sem(name):
            return ctx.enter_context(nc.semaphore(name))

        wn1x = sb("wn1x", [P, F])
        weights = sb("weights", [P, 5, F])
        we1, we2, wn1e, wn2, bn2z = (weights[:, n, :] for n in range(5))
        cols = sb("cols", [P, 4])
        be1c, be2c, wtc, btc = (cols[:, n:n + 1] for n in range(4))
        bn1b = sb("bn1b", [P, F])[:, :]
        ident = sb("ident", [P, P])
        xgT = sb("xgT", [P, RAW, C])
        ones_bf = sb("ones_bf", [P, P], BF16)
        xT_sb = sb("xT_sb", [P, NT, P])
        x_sb = sb("x_sb", [P, NT * F])      
        xw = sb("xw", [P, NT * F])
        y = sb("y", [P, NT * F])
        dst_i = sb("dst_i", [P, NCH * TPC], I32)
        dst_f = sb("dst_f", [P, NCH * TPC])
        dst_rel = sb("dst_rel", [P, NCH * TPC])
        dst_ci = sb("dst_ci", [NCH // 2, 2, C], I32)
        lo_c = sb("lo_c", [NCH // 2, 2])
        hi_c = sb("hi_c", [NCH // 2, 2])
        lo_b = sb("lo_b", [P, NCH])
        hi_b = sb("hi_b", [P, NCH])
        span = sb("span", [P, NCH])
        base_i = sb("base_i", [P, NCH], I32)
        widest = sb("widest", [P, 1])
        last_lo = sb("last_lo", [P, 1])
        is_late = sb("is_late", [P, 1])
        narrow_i = sb("narrow_i", [P, 1], I32)
        iota_i = sb("iota_i", [P, WW], I32)
        iota_f = sb("iota_f", [P, WW])
        window_i = sb("window_i", [P, NW], I32)
        window_f = sb("window_f", [P, NW])
        idx = sb("idx", [P, IDX_RING, 2 * TPC], I32)
        ea = sb("ea", [P, EA_RING, C])
        ew = sb("ew", [P, EW_RING, C])
        gath = sb("gath", [P, U, C])
        h1 = sb("h1", [P, 2, C])
        tw = sb("tw", [P, 2, C])
        ef = sb("ef", [P, 2, C])
        pre = sb("pre", [P, 2, C])
        r = sb("r", [P, 2, C])
        hot = sb("hot", [P, 2, TPC, W])
        hot_count = sb("hot_count", [P, 2, TPC, W], BF16)
        hot_wide = sb("hot_wide", [P, 2, WW])
        acc = sb("acc", [P, NPAD])
        degree = sb("degree", [P, NPAD])
        ysum = sb("ysum", [P, NT])
        nmean = sb("nmean", [P, NT])
        square = sb("square", [P, 4, F])
        ssq = sb("ssq", [P, NT])
        std = sb("std", [P, NT])
        rstd = sb("rstd", [P, NT])
        eps = sb("eps", [P, 1])

        ps = ctx.enter_context(nc.psum_tensor("ps", [P, 8, 512], F32))
        ps_a, ps_n = ps[:, 0, :], ps[:, 1, :]
        ps_b, ps_c, ps_d = (ps[:, 2 * n:2 * n + 2, :] for n in range(1, 4))

        w_in = sem("w_in")
        xT_in = [sem(f"xT_in{n}") for n in range(4)]
        wn1_in = sem("wn1_in")
        late_in = sem("late_in")
        rows_in = sem("rows_in")
        ident_zero = sem("ident_zero")
        ident_ready = sem("ident_ready")
        xg_ready = sem("xg_ready")
        xg_copied = sem("xg_copied")
        dst_in = [sem("dst_rows_in"), sem("dst_tiles_in")]
        consts = sem("consts")
        iota_done = sem("iota_done")
        acc_zero = sem("acc_zero")
        xw_ready = sem("xw_ready")
        xw_copied = sem("xw_copied")
        table_out = sem("table_out")
        span_ready = sem("span_ready")
        span_out = sem("span_out")
        span_in = sem("span_in")
        dve_prep = sem("dve_prep")
        flag_ready = sem("flag_ready")
        idx_in = [sem(f"idx_in{n}") for n in range(IDX_RING)]
        ea_in = [sem(f"ea_in{n}") for n in range(EA_RING)]
        ew_in = [sem(f"ew_in{n}") for n in range(EW_RING)]
        gath_in = [sem(f"gath_in{n}") for n in range(U)]
        tables_ready = sem("tables_ready")
        slots_granted = sem("slots_granted")
        a_ready = sem("a_ready")
        h1_ready = sem("h1_ready")
        b_ready = sem("b_ready")
        tw_ready = sem("tw_ready")
        ef_ready = sem("ef_ready")
        c_ready = sem("c_ready")
        pre_ready = sem("pre_ready")
        r_ready = sem("r_ready")
        hot_ready = sem("hot_ready")
        d_ready = sem("d_ready")
        hot_count_ready = sem("hot_count_ready")
        count_ready = sem("count_ready")
        count_added = sem("count_added")
        acc_done = sem("acc_done")
        wide_ready = sem("wide_ready")
        wide_used = sem("wide_used")
        wide_sum = sem("wide_sum")
        wide_added = sem("wide_added")
        msg_ready = sem("msg_ready")
        y_ready = sem("y_ready")
        nmean_ready = sem("nmean_ready")
        ssq_ready = sem("ssq_ready")
        std_ready = sem("std_ready")
        rstd_ready = sem("rstd_ready")
        norm_ready = [sem(f"norm_ready{g}") for g in range(len(GROUPS))]
        out_done = sem("out_done")

        block = ctx.enter_context(nc.Block())

        src_v = src.rearrange("p (n t) -> p n t", t=2 * TPC)
        ea_v = edge_attr.rearrange("p (n c) -> p n c", c=C)
        x_rows, out_rows, table_rows = (a.rearrange("(j p) f -> p j f", p=P) for a in (x, out, table))
        groups = list(enumerate(GROUPS))

        xT_parts = [(0, 4), (4, 12), (12, 20), (20, NT)]

        def group_cols(js):
            return slice(js[0] * F, (js[-1] + 1) * F)

        def by_tile(a):
            return a.rearrange("p (j f) -> p j f", f=F)

        def tiles_in(bank, js):
            return [bank[:, n * F:(n + 1) * F] for n in range(len(js))]

        last_out = [ps[:, n, 0:F] for n in range(len(GROUPS[-1]))]

        def normalise(engine, js):
            for j in js:
                at = y[:, j * F:(j + 1) * F]
                g = [j in group for group in GROUPS].index(True)
                engine.tensor_scalar(at, at, nmean[:, j:j + 1], rstd[:, j:j + 1], ALU.add, ALU.mult
                                     ).then_inc(norm_ready[g], 1)

        @block.sync
        def _(sp):
            sp.dma_start(idx[:, 0, :], src_v[:, 0, :]).then_inc(idx_in[0], 16)
            sp.dma_start(wn1x[:, :], Wn1x).then_inc(wn1_in, 16)
            for n, (a, b) in enumerate(xT_parts):
                sp.dma_start(xT_sb[:, a:b, :], xT[:, a * P:b * P].rearrange("f (j p) -> f j p", p=P)
                             ).then_inc(xT_in[n], 16)
                if n == 0:
                    sp.dma_start(dst_ci[:, :, :], dst_rows).then_inc(dst_in[0], 16)
                if n == 1:
                    sp.dma_start(idx[:, 1, :], src_v[:, 1, :]).then_inc(idx_in[1], 16)
            sp.dma_start(dst_i[:, :], dst).then_inc(dst_in[1], 16)
            sp.wait_ge(span_ready, 2)
            for n, part in enumerate((lo_c, hi_c)):
                sp.dma_start(span_dram[n, :].rearrange("(p a) -> p a", a=2), part[:, :]).then_inc(span_out, 16)
            sp.wait_ge(span_out, 32)
            for n, part in enumerate((lo_b, hi_b)):
                sp.dma_start(part[:, :], span_dram[n:n + 1, :].partition_broadcast(P)).then_inc(span_in, 16)
            sp.wait_ge(xw_copied, len(groups))

            def load_indices(turn, q):
                pair = turn * IDX_RING + q
                if not isinstance(turn, int) or turn:
                    for slot in (2 * q, 2 * q + 1):
                        sp.wait_ge(gath_in[slot], turn * (16 * TPC))
                sp.dma_start(idx[:, q, :], src_v[:, bass.ds(pair, 1), :]).then_inc(idx_in[q], 16)

            def load_pair(pair, slot):
                wait_count(sp, a_ready, 2 * (pair - EA_RING) + 2)
                sp.dma_start(ea[:, slot, :], ea_v[:, bass.ds(pair, 1), :]).then_inc(ea_in[slot], 16)
                for n in range(2):
                    c = pair * 2 + n
                    wait_count(sp, tw_ready, c - EW_RING + 1)
                    sp.dma_start(ew[:, 2 * slot + n, :], edge_weight[:, bass.ds(c * C, C)].partition_broadcast(P)
                                 ).then_inc(ew_in[2 * slot + n], 16)

            load_indices(0, 2)
            sp.wait_ge(table_out, 16 * len(groups))
            load_pair(0, 0)
            load_indices(0, 3)
            load_pair(1, 1)
            load_indices(1, 0)
            load_pair(2, 0)
            load_indices(1, 1)
            load_pair(3, 1)
            with sp.Fori(1, NCH // U - 1) as turn:
                for q in range(IDX_RING):
                    load_indices(turn + (q + IDX_LEAD) // IDX_RING, (q + IDX_LEAD) % IDX_RING)
                    load_pair(turn * IDX_RING + q, q % EA_RING)
            for pair in range((NCH // U - 1) * IDX_RING, NCH // 2):
                if pair + IDX_LEAD < NCH // 2:
                    load_indices((pair + IDX_LEAD) // IDX_RING, (pair + IDX_LEAD) % IDX_RING)
                load_pair(pair, pair % EA_RING)
            for g, js in groups:
                sp.wait_ge(norm_ready[g], len(js))
                sp.dma_start(out_rows[:, js[0]:js[-1] + 1, :], by_tile(y[:, group_cols(js)])).then_inc(out_done, 16)
            sp.wait_ge(out_done, 16 * len(groups))

        @block.gpsimd
        def _(pool):
            nc.gpsimd.memset(ident[:, :], 0.0).then_inc(ident_zero, 1)
            pool.wait_ge(ident_zero, 1)
            nc.gpsimd.affine_select(out=ident[:, :], in_=ident[:, :], compare_op=ALU.not_equal, fill=1.0,
                                    base=0, pattern=[[-1, P]], channel_multiplier=1).then_inc(ident_ready, 1)
            nc.gpsimd.iota(iota_i[:, :], pattern=[[1, WW]], base=0, channel_multiplier=0).then_inc(iota_done, 1)
            nc.gpsimd.iota(window_i[:, :], pattern=[[WW, NW]], base=0, channel_multiplier=0).then_inc(iota_done, 1)

            def gather(turn, u):
                c = turn * U + u
                if u % 2 == 0:
                    pool.wait_ge(idx_in[u // 2], (turn + 1) * 16)
                if isinstance(c, int) and U <= c < U + RAW:
                    pool.wait_ge(xg_ready, c - U + 1)
                else:
                    wait_count(pool, pre_ready, c - U + 1)
                pool.sem_inc(slots_granted, 1)
                tiles = tiles_of(c)
                for t in range(tiles):
                    at = TPC * (u % 2) + t
                    pool.indirect_dma_start(
                        gath[:, u, t * F:(t + 1) * F], None, x if isinstance(c, int) and c < RAW else table,
                        bass.IndirectOffsetOnAxis(idx[:, u // 2, at:at + 1], 0)).then_inc(gath_in[u], 16)

            for c in range(U + RAW):
                if c == RAW:
                    pool.wait_ge(table_out, 16 * len(groups))
                gather(c // U, c % U)
            with pool.Fori(1, NCH // U - 1) as turn:
                for u in range(RAW, U + RAW):
                    gather(turn + u // U, u % U)
            for c in range((NCH // U - 1) * U + RAW, NCH):
                gather(c // U, c % U)
            for n, js in enumerate((BATCHES[0][-DVE_LATE - POOL_TILES:-DVE_LATE], BATCHES[1][-1:])):
                pool.wait_ge(rstd_ready, n + 1)
                normalise(nc.gpsimd, js)

        @block.scalar
        def _(act):
            act.wait_ge(consts, 2)
            nc.scalar.activation(std[:, 0:1], eps[:, :], ACT.Sigmoid).then_inc(tables_ready, 1)
            act.dma_start(bn1b, rows.rearrange("(a n) -> a n", a=1).partition_broadcast(P)
                          ).then_inc(rows_in, 16)
            act.wait_ge(xT_in[0], 16)
            act.dma_start(weights[:, :, :], weights_in).then_inc(w_in, 16)
            act.dma_start(cols[:, :], columns).then_inc(w_in, 16)
            for g, js in groups:
                act.wait_ge(xw_copied, g + 1)
                act.dma_start(table_rows[:, js[0]:js[-1] + 1, :], by_tile(xw[:, group_cols(js)])
                              ).then_inc(table_out, 16)
            for c in range(RAW):
                act.wait_ge(xg_ready, c + 1)
                nc.scalar.activation(xgT[:, c, :], ps[:, (7 + c) % 8, :], ACT.Copy).then_inc(xg_copied, 1)
            act.wait_ge(w_in, 32)

            def squares(g):
                for j in GROUPS[g]:
                    act.wait_ge(nmean_ready, j + 1)
                    wait_count(act, ssq_ready, j - 3)
                    nc.scalar.activation(square[:, j % 4, :], y[:, j * F:(j + 1) * F], ACT.Square,
                                         bias=nmean[:, j:j + 1], accum_out=ssq[:, j:j + 1]).then_inc(ssq_ready, 1)

            def deviations(n):
                js = BATCHES[n]
                act.wait_ge(ssq_ready, js[-1] + 1)
                nc.scalar.activation(std[:, js[0]:js[-1] + 1], ssq[:, js[0]:js[-1] + 1], ACT.Sqrt,
                                     bias=eps[:, 0:1], scale=1.0 / F).then_inc(std_ready, 1)

            def step(turn, u):
                k = turn * U + u
                if isinstance(k, int) and k == U - 1:
                    act.dma_start(by_tile(x_sb[:, :]), x_rows).then_inc(late_in, 16)
                if not isinstance(k, int) or k >= 0:
                    act.wait_ge(pre_ready, k + 1)
                    wait_count(act, d_ready, k - 1)
                    n = tiles_of(k) * F
                    nc.scalar.activation(r[:, u % 2, 0:n], pre[:, u % 2, 0:n], ACT.Relu).then_inc(r_ready, 1)
                c = k + 3
                if not isinstance(c, int) or 0 <= c < NCH:
                    s = (u + 3) % EW_RING
                    act.wait_ge(ew_in[s], (turn * (U // EW_RING) + (u + 3) // EW_RING + 1) * 16)
                    wait_count(act, ef_ready, c - 1)
                    nc.scalar.activation(tw[:, s % 2, :], ew[:, s, :], ACT.Sigmoid, bias=btc, scale=wtc
                                         ).then_inc(tw_ready, 1)
                    act.wait_ge(a_ready, c + 1)
                    wait_count(act, b_ready, c - 1)
                    nc.scalar.activation(h1[:, s % 2, :], ps_a, ACT.Relu, bias=be1c
                                         ).then_inc(h1_ready, 1)

            def narrow(turn, u):
                step(turn, u)
                k = turn * U + u
                if isinstance(k, int) and early_group(k - 2):
                    squares(k - 2 - (NCH - EARLY_CHUNKS))
                if isinstance(k, int) and k == NCH - LEAD:
                    deviations(0)

            act.wait_ge(flag_ready, 1)
            is_narrow = nc.scalar.value_load(narrow_i[0:1, 0:1], min_val=0, max_val=1)
            with act.If(is_narrow):
                main_steps(act, narrow)
            with act.Else():
                main_steps(act, step)
                for g in range(len(GROUPS) - 1):
                    squares(g)
                deviations(0)
            squares(len(GROUPS) - 1)
            deviations(1)

        @block.tensor
        def _(pe):
            pe.wait_ge(wn1_in, 16)
            for g, js in groups:
                for j in js:
                    o = ps[:, g, (j - js[0]) * F:(j - js[0] + 1) * F]
                    for n, (first, _) in enumerate(xT_parts):
                        if j == first:
                            pe.wait_ge(xT_in[n], 16)
                    last = nc.tensor.matmul(o, xT_sb[:, j, :], wn1x[:, :], start=True, stop=True)
                last.then_inc(xw_ready, 1)
            pe.wait_ge(ident_ready, 1)
            for c in range(RAW):
                pe.wait_ge(gath_in[c], 16 * TPC)
                wait_count(pe, xw_copied, c)
                for t in range(TPC):
                    last = nc.tensor.transpose(ps[:, (7 + c) % 8, t * P:(t + 1) * P],
                                               gath[:, c, t * F:(t + 1) * F], ident[:, :])
                last.then_inc(xg_ready, 1)
            pe.wait_ge(w_in, 32)
            pe.wait_ge(consts, 1)
            pe.wait_ge(xw_copied, len(groups))
            pe.wait_ge(xg_copied, RAW)

            def front(turn, u):
                k = turn * U + u
                c = k + 3
                if not isinstance(c, int) or 0 <= c < NCH:
                    s, pair = (u + 3) % 2, (u + 3) // 2
                    if s == 0:
                        pe.wait_ge(ea_in[pair % EA_RING], (turn * (IDX_RING // EA_RING) + pair // EA_RING + 1) * 16)
                    wait_count(pe, h1_ready, c)
                    rows = slice(EF * s, EF * s + EF)
                    nc.tensor.matmul(ps_a, we1[rows, :], ea[rows, pair % EA_RING, :], start=True, stop=True
                                     ).then_inc(a_ready, 1)
                c = k + 2
                if not isinstance(c, int) or 0 <= c < NCH:
                    pe.wait_ge(h1_ready, c + 1)
                    wait_count(pe, ef_ready, c - 1)
                    nc.tensor.matmul(ps_b[:, u % 2, :], we2, h1[:, u % 2, :], start=True, stop=True
                                     ).then_inc(b_ready, 1)
                c = k + 1
                if not isinstance(c, int) or 0 <= c < NCH:
                    b = (u + 1) % 2
                    pe.wait_ge(ef_ready, c + 1)
                    wait_count(pe, pre_ready, c - 1)
                    raw = isinstance(c, int) and c < RAW
                    for t in range(tiles_of(c)):
                        last = nc.tensor.matmul(ps_c[:, b, t * F:(t + 1) * F], ef[:, b, t * P:(t + 1) * P],
                                                wn1e, start=True, stop=not raw)
                        if raw:
                            last = nc.tensor.matmul(ps_c[:, b, t * F:(t + 1) * F], xgT[:, c, t * P:(t + 1) * P],
                                                    wn1x[:, :], start=False, stop=True)
                    last.then_inc(c_ready, 1)

            def degree_product(j, o):
                nc.tensor.matmul(o, degree[:, j * P:(j + 1) * P], bn2z, start=True, stop=False)

            def sum_product(j, o):
                nc.tensor.matmul(o, acc[:, j * P:(j + 1) * P], wn2, start=False, stop=True).then_inc(msg_ready, 1)

            def node_products(js, bank):
                for j, o in zip(js, tiles_in(bank, js)):
                    degree_product(j, o)
                    sum_product(j, o)

            def count(c, slot):
                slot = c % 2 if isinstance(c, int) else slot
                pe.wait_ge(hot_count_ready, c + 1)
                wait_count(pe, count_added, c)
                for t in range(tiles_of(c)):
                    last = nc.tensor.matmul(ps_n[:, 0:W], ones_bf[:, :], hot_count[:, slot, t, :],
                                            start=(t == 0), stop=(t == tiles_of(c) - 1))
                last.then_inc(count_ready, 1)

            def narrow(turn, u):
                front(turn, u)
                k = turn * U + u
                counted = counted_at(k)
                for c in counted[:1]:
                    count(c, (u + LEAD) % 2)
                if isinstance(k, int) and k < 0:
                    return
                b, tiles = u % 2, tiles_of(k)
                pe.wait_ge(r_ready, k + 1)
                pe.wait_ge(hot_ready, k + 1)
                wait_count(pe, acc_done, k - 1)
                if early_group(k - 1):
                    pe.wait_ge(y_ready, early_group(k - 1)[-1] + 1)
                for t in range(tiles):
                    last = nc.tensor.matmul(ps_d[:, b, 0:W], r[:, b, t * F:(t + 1) * F], hot[:, b, t, :],
                                            start=(t == 0), stop=(t == tiles - 1))
                last.then_inc(d_ready, 1)
                for c in counted[1:]:
                    count(c, None)
                if early_group(k):
                    pe.wait_ge(acc_done, k)
                    node_products(early_group(k), ps_d[:, 1 - b, :])

            def general(turn, u):
                front(turn, u)
                k = turn * U + u
                if isinstance(k, int) and k < 0:
                    return
                b, tiles = u % 2, tiles_of(k)
                with pe.Fori(0, NW) as w:
                    pe.wait_ge(r_ready, k + 1)
                    pe.wait_ge(wide_added, k * NW + w + 1)
                    for t in range(tiles):
                        pe.wait_ge(wide_ready, (k * NW) * TPC + w * tiles + t + 1)
                        nc.tensor.matmul(ps_d[:, 0, 0:WW], r[:, b, t * F:(t + 1) * F], hot_wide[:, t % 2, :],
                                         start=(t == 0), stop=(t == tiles - 1))
                        hot_bf = hot_wide[:, t % 2, :].bitcast(BF16)[:, 1::2]
                        last = nc.tensor.matmul(ps_d[:, 1, 0:WW], ones_bf[:, :], hot_bf,
                                                start=(t == 0), stop=(t == tiles - 1))
                        last.then_inc(wide_used, 1)
                    nc.tensor.drain().then_inc(wide_sum, 1)
                nc.tensor.drain().then_inc(d_ready, 1)

            pe.wait_ge(flag_ready, 1)
            is_narrow = nc.tensor.value_load(narrow_i[0:1, 0:1], min_val=0, max_val=1)
            with pe.If(is_narrow):
                main_steps(pe, narrow)
                pe.wait_ge(count_added, NCH)
                pe.wait_ge(ef_ready, NCH)
                for j, o in zip(GROUPS[-1], last_out):
                    degree_product(j, o)
                pe.wait_ge(acc_done, NCH)
            with pe.Else():
                main_steps(pe, general)
                pe.wait_ge(acc_done, NCH)
                pe.wait_ge(count_added, NCH)
                for g, js in groups[:-1]:
                    node_products(js, ps[:, g, :])
                pe.wait_ge(y_ready, EARLY)
                for j, o in zip(GROUPS[-1], last_out):
                    degree_product(j, o)
            for j, o in zip(GROUPS[-1], last_out):
                sum_product(j, o)

        @block.vector
        def _(dve):
            def measure_spans():
                dve.wait_ge(dst_in[1], 16)
                nc.vector.tensor_copy(dst_f[:, :], dst_i[:, :]).then_inc(dve_prep, 1)
                dve.wait_ge(iota_done, 2)
                nc.vector.tensor_copy(iota_f[:, :], iota_i[:, :]).then_inc(dve_prep, 1)
                nc.vector.tensor_copy(window_f[:, :], window_i[:, :]).then_inc(dve_prep, 1)
                nc.vector.memset(acc[:, :], 0.0).then_inc(acc_zero, 1)
                dve.wait_ge(span_in, 32)
                nc.vector.tensor_tensor(span[:, :], hi_b[:, :], lo_b[:, :], ALU.subtract).then_inc(dve_prep, 1)
                nc.vector.tensor_copy(base_i[:, :], lo_b[:, :]).then_inc(dve_prep, 1)
                dve.wait_ge(dve_prep, 5)
                nc.vector.tensor_reduce(widest[:, :], span[:, :], axis=AXX, op=ALU.max).then_inc(dve_prep, 1)
                nc.vector.tensor_tensor(dst_rel[:, :].rearrange("p (c t) -> p c t", t=TPC),
                                        dst_f[:, :].rearrange("p (c t) -> p c t", t=TPC),
                                        lo_b[:, :].unsqueeze(2).broadcast_to([P, NCH, TPC]), ALU.subtract
                                        ).then_inc(dve_prep, 1)
                nc.vector.tensor_reduce(last_lo[:, :], lo_b[:, NCH - EARLY_CHUNKS:], axis=AXX, op=ALU.min
                                        ).then_inc(dve_prep, 1)
                dve.wait_ge(dve_prep, 8)
                nc.vector.tensor_scalar(is_late[:, :], last_lo[:, :], float(EARLY * P), None, ALU.is_ge
                                        ).then_inc(dve_prep, 1)
                dve.wait_ge(dve_prep, 9)
                nc.vector.tensor_scalar(narrow_i[:, :], widest[:, :], float(W), is_late[:, :], ALU.is_lt, ALU.mult
                                        ).then_inc(flag_ready, 1)

            nc.vector.memset(ones_bf[:, :], 1.0).then_inc(consts, 1)
            nc.vector.memset(eps[:, :], EPS).then_inc(consts, 1)
            nc.vector.memset(degree[:, :], 0.0).then_inc(acc_zero, 1)
            dve.wait_ge(dst_in[0], 16)
            nc.vector.tensor_reduce(lo_c[:, :], dst_ci[:, :, :], axis=AXX, op=ALU.min).then_inc(span_ready, 1)
            nc.vector.tensor_reduce(hi_c[:, :], dst_ci[:, :, :], axis=AXX, op=ALU.max).then_inc(span_ready, 1)
            dve.wait_ge(rows_in, 16)
            for g, js in groups:
                dve.wait_ge(xw_ready, g + 1)
                nc.vector.tensor_tensor(
                    xw[:, group_cols(js)].rearrange("p (j f) -> p j f", f=F),
                    ps[:, g, 0:len(js) * F].rearrange("p (j f) -> p j f", f=F),
                    bn1b.unsqueeze(1).broadcast_to([P, len(js), F]), ALU.add).then_inc(xw_copied, 1)
            measure_spans()
            dve.wait_ge(w_in, 32)
            dve.wait_ge(acc_zero, 2)
            dve.wait_ge(flag_ready, 1)

            def gate(turn, u):
                c = turn * U + u + 2
                if not isinstance(c, int) or 0 <= c < NCH:
                    b = u % 2
                    dve.wait_ge(b_ready, c + 1)
                    dve.wait_ge(tw_ready, c + 1)
                    wait_count(dve, c_ready, c - 1)
                    nc.vector.scalar_tensor_tensor(ef[:, b, :], ps_b[:, b, :], be2c, tw[:, b, :],
                                                   op0=ALU.add, op1=ALU.mult).then_inc(ef_ready, 1)

            def add_gathered(turn, u):
                c = turn * U + u + 1
                if not isinstance(c, int) or 0 <= c < NCH:
                    s, t, tiles = (u + 1) % U, turn + (u + 1) // U, tiles_of(c)
                    dve.wait_ge(c_ready, c + 1)
                    wait_count(dve, r_ready, c - 1)
                    if isinstance(c, int) and c < RAW:
                        nc.vector.tensor_tensor(pre[:, s % 2, :].rearrange("p (t f) -> p t f", f=F),
                                                ps_c[:, s % 2, :].rearrange("p (t f) -> p t f", f=F),
                                                bn1b.unsqueeze(1).broadcast_to([P, TPC, F]), ALU.add
                                                ).then_inc(pre_ready, 1)
                        return
                    dve.wait_ge(gath_in[s], t * (16 * TPC) + 16 * tiles)
                    nc.vector.tensor_tensor(pre[:, s % 2, 0:tiles * F], ps_c[:, s % 2, 0:tiles * F],
                                            gath[:, s, 0:tiles * F], ALU.add).then_inc(pre_ready, 1)

            def combine(js, products):
                dve.wait_ge(late_in, 16)
                dve.wait_ge(msg_ready, js[-1] + 1)
                for j, product in zip(js, products):
                    nc.vector.scalar_tensor_tensor(
                        y[:, j * F:(j + 1) * F], x_sb[:, j * F:(j + 1) * F], 2.0,
                        product, op0=ALU.mult, op1=ALU.add,
                        accum_out=ysum[:, j:j + 1]).then_inc(y_ready, 1)

            def negate_means(js):
                dve.wait_ge(y_ready, js[-1] + 1)
                nc.vector.tensor_scalar(nmean[:, js[0]:js[-1] + 1], ysum[:, js[0]:js[-1] + 1], -1.0 / F, None,
                                        ALU.mult).then_inc(nmean_ready, len(js))

            def invert(n):
                js = BATCHES[n]
                dve.wait_ge(std_ready, n + 1)
                nc.vector.reciprocal(rstd[:, js[0]:js[-1] + 1], std[:, js[0]:js[-1] + 1]).then_inc(rstd_ready, 1)

            def one_hot(rows, c):
                return nc.vector.tensor_tensor(
                    rows, iota_f[:, 0:W].unsqueeze(1).broadcast_to([P, TPC, W]),
                    dst_rel[:, bass.ds(c * TPC, TPC)].unsqueeze(2).broadcast_to([P, TPC, W]), ALU.is_equal)

            def one_hot_count(c, slot):
                one_hot(hot_count[:, slot, :, :], c).then_inc(hot_count_ready, 1)

            def add_count(c, count_base, next_slot):
                dve.wait_ge(count_ready, c + 1)
                wait_count(dve, count_added, c)
                window = degree[:, bass.ds(count_base, W)]
                nc.vector.tensor_tensor(window, window, ps_n[:, 0:W], ALU.add).then_inc(count_added, 1)
                if not isinstance(c, int) or c + 1 < NCH:
                    one_hot_count(c + 1, (c + 1) % 2 if isinstance(c, int) else next_slot)

            def narrow_step(turn, u, base, count_bases):
                k = turn * U + u
                done = early_group(k - 1)
                if done:
                    combine(done, tiles_in(ps_d[:, u % 2, :], done))
                gate(turn, u)
                counted = list(zip(counted_at(k), count_bases))
                for c, count_base in counted[:1]:
                    add_count(c, count_base, (u + LEAD + 1) % 2)
                c = k + 1
                if not isinstance(c, int) or 0 <= c < NCH:
                    wait_count(dve, d_ready, c - 1)
                    one_hot(hot[:, (u + 1) % 2, :, :], c).then_inc(hot_ready, 1)
                add_gathered(turn, u)
                if done:
                    negate_means(done)
                if isinstance(k, int) and k == NCH - 2:
                    invert(0)
                if isinstance(k, int) and k == NCH - 1:
                    dve.wait_ge(rstd_ready, 1)
                    normalise(nc.vector, BATCHES[0][:DVE_SOON])
                if not isinstance(k, int) or k >= 0:
                    dve.wait_ge(d_ready, k + 1)
                    wait_count(dve, acc_done, k)
                    window = acc[:, bass.ds(base, W)]
                    nc.vector.tensor_tensor(window, window, ps_d[:, u % 2, 0:W], ALU.add).then_inc(acc_done, 1)
                for c, count_base in counted[1:]:
                    add_count(c, count_base, None)

            def bases(first, n):
                return nc.values_load_multi_w_load_instructions(
                    base_i[0:1, bass.ds(first, n)], engines=[mybir.EngineType.DVE],
                    min_val=0, max_val=NPAD - W,
                    skip_runtime_bounds_check_because="a destination is a node or the padding value")[1]

            def general_step(turn, u):
                gate(turn, u)
                add_gathered(turn, u)
                k = turn * U + u
                if isinstance(k, int) and k < 0:
                    return
                tiles = tiles_of(k)
                with dve.Fori(0, NW) as w:
                    for t in range(tiles):
                        dve.wait_ge(wide_used, (k * NW) * TPC + w * tiles + t + 1)
                        at = k * TPC + t
                        nc.vector.tensor_scalar(hot_wide[:, t % 2, :], iota_f[:, :], window_f[:, bass.ds(w, 1)],
                                                dst_f[:, bass.ds(at, 1)], ALU.add, ALU.is_equal
                                                ).then_inc(wide_ready, 1)
                    dve.wait_ge(wide_sum, k * NW + w + 1)
                    for n, total in enumerate((acc, degree)):
                        window = total[:, bass.ds(w * WW, WW)]
                        last = nc.vector.tensor_tensor(window, window, ps_d[:, n, 0:WW], ALU.add)
                    last.then_inc(wide_added, 1)
                nc.vector.drain().then_inc(acc_done, 1)
                nc.vector.drain().then_inc(count_added, 1)

            is_narrow = nc.vector.value_load(narrow_i[0:1, 0:1], min_val=0, max_val=1)
            with dve.If(is_narrow):
                one_hot_count(0, 0)

                def peeled(k):
                    narrow_step(k // U, k % U, bases(k, 1)[0] if k >= 0 else None,
                                [bases(c, 1)[0] for c in counted_at(k)])

                for k in range(-LEAD, U):
                    peeled(k)
                with dve.Fori(1, TURNS) as turn:
                    at, count_at = bases(turn * U, U), bases(turn * U + LEAD, U)
                    for u in range(U):
                        narrow_step(turn, u, at[u], [count_at[u]])
                for k in range(TURNS * U, NCH):
                    peeled(k)
                normalise(nc.vector, BATCHES[0][DVE_SOON:-DVE_LATE - POOL_TILES])
            with dve.Else():
                nc.vector.drain().then_inc(wide_used, 2)
                nc.vector.drain().then_inc(wide_added, 1)
                main_steps(dve, general_step)
                for g, js in groups[:-1]:
                    combine(js, tiles_in(ps[:, g, :], js))
                    negate_means(js)
                invert(0)
                dve.wait_ge(rstd_ready, 1)
                normalise(nc.vector, BATCHES[0][:-DVE_LATE - POOL_TILES])
            for j, o in zip(GROUPS[-1], last_out):
                combine([j], [o])
                negate_means([j])
            normalise(nc.vector, BATCHES[0][-DVE_LATE:])
            invert(1)
            dve.wait_ge(rstd_ready, 2)
            normalise(nc.vector, BATCHES[1][:-1])


def kernel(x, src, dst, edge_attr_64, edge_weight, L0_gnn_We1, L0_gnn_be1, L0_gnn_We2, L0_gnn_be2, L0_gnn_Wt,
           L0_gnn_bt, L0_gnn_Wn1, L0_gnn_bn1, L0_gnn_Wn2, L0_gnn_bn2):
    import concourse.bacc as bacc
    from concourse.bass_utils import run_bass_kernel_spmd

    def padded(a, rows, value=0):
        a = np.asarray(a)
        whole = np.full((rows,) + a.shape[1:], value, a.dtype)
        whole[:a.shape[0]] = a
        return whole

    xp = padded(x, NPAD)
    dp = padded(dst, EPAD, N_NODES)
    ep = padded(edge_attr_64, EPAD).reshape(NCH // 2, 2, C, EF)
    host = {
        "x": xp,
        "xT": xp.T,
        "src": padded(src, EPAD).reshape(NCH * TPC, P).T,
        "dst": dp.reshape(NCH * TPC, P).T,
        "dst_rows": dp.reshape(NCH // 2, 2, C),
        "edge_attr": ep.transpose(1, 3, 0, 2).reshape(2 * EF, NCH // 2 * C),
        "edge_weight": padded(edge_weight, EPAD).reshape(1, EPAD),
        "Wn1x": np.asarray(L0_gnn_Wn1)[:F],
        "weights": np.stack([np.concatenate([L0_gnn_We1, L0_gnn_We1]), L0_gnn_We2, np.asarray(L0_gnn_Wn1)[F:],
                             L0_gnn_Wn2, padded(np.asarray(L0_gnn_bn2)[None], P)], axis=1),
        "columns": np.stack([L0_gnn_be1, L0_gnn_be2, np.asarray(L0_gnn_Wt)[0], L0_gnn_bt], axis=1),
        "rows": np.asarray(L0_gnn_bn1),
    }
    nc = bacc.Bacc("TRN2", target_bir_lowering=False, num_devices=1)
    arrays, args = {}, []
    for name, a in host.items():
        a = np.ascontiguousarray(a)
        arrays[f"in_{name}"] = a
        args.append(nc.dram_tensor(f"in_{name}", a.shape, mybir.dt.from_np(a.dtype), kind="ExternalInput").ap())
    args.append(nc.dram_tensor("out_y", (NPAD, F), F32, kind="ExternalOutput").ap())
    gnn_kernel(nc, *args)
    result = run_bass_kernel_spmd(nc, [arrays], core_ids=[0])
    return result.results[0]["out_y"][:N_NODES]
```
